# Optimizing a Trainium2 kernel written in Bass

```python
import numpy as np
import jax
import jax.numpy as jnp

def _softmax(x, axis=-1):
    return jax.nn.softmax(x, axis=axis)

def _gelu(x):
    return jax.nn.gelu(x, approximate=True)

def _silu(x):
    return jax.nn.silu(x)

def _sigmoid(x):
    return jax.nn.sigmoid(x)

def _layernorm(x, axis=-1, eps=1e-05):
    m = jnp.mean(x, axis=axis, keepdims=True)
    v = jnp.var(x, axis=axis, keepdims=True)
    return (x - m) / jnp.sqrt(v + eps)

def _scatter_add(tgt, idx, src, axis=0):
    return tgt.at[idx].add(src)

def _segment_sum(src, seg, n):
    return jax.ops.segment_sum(src, seg, n)
kernel_name = 'mk_gnn_preln_d2_gnn_r8_a16708'

def setup_inputs(seed: int=0):
    np.random.seed(seed)
    _w = jnp.asarray

    def _rec_inputs():
        import jax
        import jax.numpy as jnp
        _gk = jax.random.key(seed)
        x = -0.0003713 + 1 * jax.random.normal(jax.random.fold_in(_gk, 1), (12500, 256), jnp.float32)
        src = jax.random.randint(jax.random.fold_in(_gk, 2), (200000,), 0, 12500, jnp.int32)
        dst = jax.random.randint(jax.random.fold_in(_gk, 3), (200000,), 0, 12500, jnp.int32)
        _o = jnp.argsort(dst, stable=True)
        src = src[_o]
        dst = dst[_o]
        edge_weight1 = 0.000937891 + 0.999965 * jax.random.normal(jax.random.fold_in(_gk, 12), (200000, 1), jnp.float32)
        return (x, src, dst, edge_weight1)
    x, src, dst, edge_weight1 = _rec_inputs()

    def _L0_gnn_setup():
        import jax, jax.numpy as jnp
        import numpy as np
        DIM = 256
        H = 8
        HD = DIM // H
        N = 6250
        E = 100000
        FFN = 4 * DIM
        EPS = 1e-05

        def layer_norm(x, g, b):
            mu = jnp.mean(x, axis=-1, keepdims=True)
            var = jnp.mean((x - mu) ** 2, axis=-1, keepdims=True)
            return (x - mu) * jax.lax.rsqrt(var + EPS) * g + b

        def _mhsa(h, edge_bias, src, dst, Wq, Wk, Wv, Wp, bp):
            n = h.shape[0]
            Q = (h @ Wq).reshape(n, H, HD)
            K = (h @ Wk).reshape(n, H, HD)
            V = (h @ Wv).reshape(n, H, HD)
            score = jnp.einsum('ehd,ehd->eh', K[src], Q[dst]) / np.sqrt(HD) + edge_bias
            m = jax.ops.segment_max(score, dst, num_segments=n)
            ex = jnp.exp(score - m[dst])
            denom = jax.ops.segment_sum(ex, dst, num_segments=n)
            attn = ex / denom[dst]
            out = jax.ops.segment_sum(attn[:, :, None] * V[src], dst, num_segments=n)
            return out.reshape(n, DIM) @ Wp + bp
        key = jax.random.key(seed)
        ks = jax.random.split(key, 16)
        s = 1.0 / np.sqrt(DIM)
        inp = {'h': jax.random.normal(ks[0], (N, DIM), jnp.float32), 'edge_bias': jax.random.normal(ks[1], (E, 1), jnp.float32), 'src': jax.random.randint(ks[2], (E,), 0, N, jnp.int32), 'dst': jax.random.randint(ks[3], (E,), 0, N, jnp.int32), 'Wq': jax.random.normal(ks[4], (DIM, DIM), jnp.float32) * s, 'Wk': jax.random.normal(ks[5], (DIM, DIM), jnp.float32) * s, 'Wv': jax.random.normal(ks[6], (DIM, DIM), jnp.float32) * s, 'Wp': jax.random.normal(ks[7], (DIM, DIM), jnp.float32) * s, 'bp': jnp.zeros((DIM,), jnp.float32), 'ln1_g': jnp.ones((DIM,), jnp.float32), 'ln1_b': jnp.zeros((DIM,), jnp.float32), 'ln2_g': jnp.ones((DIM,), jnp.float32), 'ln2_b': jnp.zeros((DIM,), jnp.float32), 'W1': jax.random.normal(ks[8], (DIM, FFN), jnp.float32) * s, 'b1': jnp.zeros((FFN,), jnp.float32), 'W2': jax.random.normal(ks[9], (FFN, DIM), jnp.float32) * (1.0 / np.sqrt(FFN)), 'b2': jnp.zeros((DIM,), jnp.float32)}
        return inp
    _L0_gnn_all = _L0_gnn_setup()
    _L0_gnn_in = {k: v for k, v in _L0_gnn_all.items() if k in ('Wq', 'Wk', 'Wv', 'Wp', 'bp', 'ln1_g', 'ln1_b', 'ln2_g', 'ln2_b', 'W1', 'b1', 'W2', 'b2')}
    del _L0_gnn_all

    def _L1_gnn_setup():
        import jax, jax.numpy as jnp
        import numpy as np
        N_NODES = 6250
        N_EDGES = 100000
        IN_DIM = 256
        OUT_DIM = 32
        NUM_HEADS = 8
        key = jax.random.key(seed)
        ks = jax.random.split(key, 9)
        h = jax.random.normal(ks[0], (N_NODES, IN_DIM), dtype=jnp.float32)
        src = jax.random.randint(ks[1], (N_EDGES,), 0, N_NODES, dtype=jnp.int32)
        dst = jax.random.randint(ks[2], (N_EDGES,), 0, N_NODES, dtype=jnp.int32)
        s = 1.0 / np.sqrt(IN_DIM)
        W_lin = jax.random.uniform(ks[3], (IN_DIM, IN_DIM), jnp.float32, -s, s)
        b_lin = jax.random.uniform(ks[4], (IN_DIM,), jnp.float32, -s, s)
        W_gat = jax.random.normal(ks[5], (IN_DIM, NUM_HEADS * OUT_DIM), dtype=jnp.float32) * s
        attn_l = jax.random.normal(ks[6], (NUM_HEADS, OUT_DIM), dtype=jnp.float32) * 0.1
        attn_r = jax.random.normal(ks[7], (NUM_HEADS, OUT_DIM), dtype=jnp.float32) * 0.1
        gat_bias = jnp.zeros((NUM_HEADS * OUT_DIM,), dtype=jnp.float32)
        return {'h': h, 'src': src, 'dst': dst, 'W_lin': W_lin, 'b_lin': b_lin, 'W_gat': W_gat, 'attn_l': attn_l, 'attn_r': attn_r, 'gat_bias': gat_bias}
    _L1_gnn_all = _L1_gnn_setup()
    _L1_gnn_in = {k: v for k, v in _L1_gnn_all.items() if k in ('W_lin', 'b_lin', 'W_gat', 'attn_l', 'attn_r', 'gat_bias')}
    del _L1_gnn_all
    return {'x': x, 'src': src, 'dst': dst, 'edge_weight1': edge_weight1, 'L0_gnn_Wq': _L0_gnn_in['Wq'], 'L0_gnn_Wk': _L0_gnn_in['Wk'], 'L0_gnn_Wv': _L0_gnn_in['Wv'], 'L0_gnn_Wp': _L0_gnn_in['Wp'], 'L0_gnn_bp': _L0_gnn_in['bp'], 'L0_gnn_ln1_g': _L0_gnn_in['ln1_g'], 'L0_gnn_ln1_b': _L0_gnn_in['ln1_b'], 'L0_gnn_ln2_g': _L0_gnn_in['ln2_g'], 'L0_gnn_ln2_b': _L0_gnn_in['ln2_b'], 'L0_gnn_W1': _L0_gnn_in['W1'], 'L0_gnn_b1': _L0_gnn_in['b1'], 'L0_gnn_W2': _L0_gnn_in['W2'], 'L0_gnn_b2': _L0_gnn_in['b2'], 'L1_gnn_W_lin': _L1_gnn_in['W_lin'], 'L1_gnn_b_lin': _L1_gnn_in['b_lin'], 'L1_gnn_W_gat': _L1_gnn_in['W_gat'], 'L1_gnn_attn_l': _L1_gnn_in['attn_l'], 'L1_gnn_attn_r': _L1_gnn_in['attn_r'], 'L1_gnn_gat_bias': _L1_gnn_in['gat_bias']}

def reference(x, src, dst, edge_weight1, L0_gnn_Wq, L0_gnn_Wk, L0_gnn_Wv, L0_gnn_Wp, L0_gnn_bp, L0_gnn_ln1_g, L0_gnn_ln1_b, L0_gnn_ln2_g, L0_gnn_ln2_b, L0_gnn_W1, L0_gnn_b1, L0_gnn_W2, L0_gnn_b2, L1_gnn_W_lin, L1_gnn_b_lin, L1_gnn_W_gat, L1_gnn_attn_l, L1_gnn_attn_r, L1_gnn_gat_bias):
    import jax
    import jax.numpy as jnp

    def _L0_gnn_ref(h, edge_bias, src, dst, Wq, Wk, Wv, Wp, bp, ln1_g, ln1_b, ln2_g, ln2_b, W1, b1, W2, b2):
        import jax, jax.numpy as jnp
        import numpy as np
        DIM = 256
        H = 8
        HD = DIM // H
        N = 6250
        E = 100000
        FFN = 4 * DIM
        EPS = 1e-05

        def layer_norm(x, g, b):
            mu = jnp.mean(x, axis=-1, keepdims=True)
            var = jnp.mean((x - mu) ** 2, axis=-1, keepdims=True)
            return (x - mu) * jax.lax.rsqrt(var + EPS) * g + b

        def _mhsa(h, edge_bias, src, dst, Wq, Wk, Wv, Wp, bp):
            n = h.shape[0]
            Q = (h @ Wq).reshape(n, H, HD)
            K = (h @ Wk).reshape(n, H, HD)
            V = (h @ Wv).reshape(n, H, HD)
            score = jnp.einsum('ehd,ehd->eh', K[src], Q[dst]) / np.sqrt(HD) + edge_bias
            m = jax.ops.segment_max(score, dst, num_segments=n)
            ex = jnp.exp(score - m[dst])
            denom = jax.ops.segment_sum(ex, dst, num_segments=n)
            attn = ex / denom[dst]
            out = jax.ops.segment_sum(attn[:, :, None] * V[src], dst, num_segments=n)
            return out.reshape(n, DIM) @ Wp + bp
        attn_out = _mhsa(h, edge_bias, src, dst, Wq, Wk, Wv, Wp, bp)
        h1 = layer_norm(h + attn_out, ln1_g, ln1_b)
        ffn_out = jax.nn.gelu(h1 @ W1 + b1, approximate=False) @ W2 + b2
        return layer_norm(h1 + ffn_out, ln2_g, ln2_b)

    def _L1_gnn_ref(h, src, dst, W_lin, b_lin, W_gat, attn_l, attn_r, gat_bias):
        import jax, jax.numpy as jnp
        import numpy as np
        N_NODES = 6250
        N_EDGES = 100000
        IN_DIM = 256
        OUT_DIM = 32
        NUM_HEADS = 8
        N = h.shape[0]
        h = h @ W_lin + b_lin
        h_in = h
        feat = (h @ W_gat).reshape(N, NUM_HEADS, OUT_DIM)
        el = jnp.sum(feat * attn_l, axis=-1)
        er = jnp.sum(feat * attn_r, axis=-1)
        e = jax.nn.leaky_relu(el[src] + er[dst], 0.2)
        m = jax.ops.segment_max(e, dst, num_segments=N)
        m = jnp.where(jnp.isfinite(m), m, 0.0)
        e = jnp.exp(e - m[dst])
        s = jax.ops.segment_sum(e, dst, num_segments=N)
        a = e / s[dst]
        msg = feat[src] * a[:, :, None]
        out = jax.ops.segment_sum(msg, dst, num_segments=N)
        out = out.reshape(N, NUM_HEADS * OUT_DIM) + gat_bias
        out = jax.nn.leaky_relu(out, 0.01)
        return h_in + out
    h = jnp.maximum(_layernorm(x, axis=-1), 0.0)
    x = x + _L0_gnn_ref(h, edge_weight1, src, dst, L0_gnn_Wq, L0_gnn_Wk, L0_gnn_Wv, L0_gnn_Wp, L0_gnn_bp, L0_gnn_ln1_g, L0_gnn_ln1_b, L0_gnn_ln2_g, L0_gnn_ln2_b, L0_gnn_W1, L0_gnn_b1, L0_gnn_W2, L0_gnn_b2)
    h = jnp.maximum(_layernorm(x, axis=-1), 0.0)
    x = x + _L1_gnn_ref(h, src, dst, L1_gnn_W_lin, L1_gnn_b_lin, L1_gnn_W_gat, L1_gnn_attn_l, L1_gnn_attn_r, L1_gnn_gat_bias)
    return x

_drawn_inputs = setup_inputs


def setup_inputs(seed=0):
    import zlib

    import numpy as np

    out = dict(_drawn_inputs(seed))
    spreads = {'L0_gnn_bp': (0.0, 0.1),
     'L0_gnn_ln1_g': (1.0, 0.2),
     'L0_gnn_ln1_b': (0.0, 0.1),
     'L0_gnn_ln2_g': (1.0, 0.2),
     'L0_gnn_ln2_b': (0.0, 0.1),
     'L0_gnn_b1': (0.0, 0.1),
     'L0_gnn_b2': (0.0, 0.1),
     'L1_gnn_gat_bias': (0.0, 0.1)}
    factors = {'L1_gnn_attn_l': 7.546, 'L1_gnn_attn_r': 28.486}
    for name, (base, spread) in spreads.items():
        noise = np.random.default_rng([zlib.crc32(name.encode()), seed]).standard_normal(out[name].shape)
        drawn = base * np.exp(spread * noise) if base else spread * noise
        out[name] = jnp.asarray(drawn.astype(out[name].dtype))
    for name, factor in factors.items():
        out[name] = (out[name] * factor).astype(out[name].dtype)
    return out
```

```python
from contextlib import ExitStack

import concourse.bass as bass
from concourse import mybir

F32 = mybir.dt.float32
I32 = mybir.dt.int32
ALU = mybir.AluOpType
ACT = mybir.ActivationFunctionType
AXX = mybir.AxisListType.X

P = 128
N, D, H, E = 12500, 256, 8, 200000
HD = D // H
FFN = 4 * D
FC = FFN // P
NT = -(-N // P)
NPAD = NT * P
SPAN = 2 * P
NSPAN = -(-E // SPAN)
ST = 8
CH = 2 * ST
NB = -(-(NSPAN + NT) // ST)
NS = NB * ST
LC = -(-NSPAN // P)
HV = H * (HD + 1)
KVW = D + HV
FTW = HV + H
BIG = 1.0e30
EPS = 1e-5
NOWHERE = 1 << 20
assert NB % 2 == 0 and NB >= 6 and NS > NSPAN + NT - 1


class Chain:

    def __init__(self, eng, sem, per):
        self.eng, self.sem, self.per, self.k, self.n = eng, sem, per, 0, 0

    def start(self, n):
        self.k, self.n = 0, n

    def did(self, ins):
        ins.then_inc(self.sem, 1)
        self.k += 1

    def sync(self):
        self.eng.wait_ge(self.sem, self.n * self.per + self.k)

    def seq(self, ins):
        self.did(ins)
        self.sync()

    def end(self):
        assert self.k == self.per, (self.k, self.per)


def wait(eng, sem, count):
    if isinstance(count, int) and count <= 0:
        return
    eng.wait_ge(sem, count)


def build(nc, x, last, edges, Wq, Wk, Wv, Wp, bp, g1, b1n, g2, b2n, W1, b1, W2, b2,
          Wl, bl, Wg, al, ar, gb, out):
    ctx = ExitStack()
    with ctx:
        def sb(name, shape, dt=F32):
            return ctx.enter_context(nc.sbuf_tensor(name, shape, dt))

        def sem(name):
            return ctx.enter_context(nc.semaphore(name))

        def dram(name, shape):
            return nc.dram_tensor(name, shape, F32, kind="Internal").ap()

        kv_tab = dram("kv_tab", (NPAD, KVW))
        q_tab = dram("q_tab", (NPAD, D))
        h_tab = dram("h_tab", (NPAD, D))
        ft_tab = dram("ft_tab", (NPAD, FTW))
        er_tab = dram("er_tab", (NPAD, H))
        xh_tab = dram("xh_tab", (NPAD, D))
        sums = dram("sums", (NS * P, HV))

        ident = sb("ident", [P, P])
        ones = sb("ones", [P, P])
        lane = sb("lane", [P, P])
        steps = sb("steps", [P, NS])
        spanid = sb("spanid", [P, LC])
        tile_of = sb("tile_of", [P, NS])
        same = sb("same", [P, NS])
        tile_row = sb("tile_row", [1, NS], I32)
        endstep = sb("endstep", [1, NT], I32)
        endf = sb("endf", [1, NT])
        last_i = sb("last_i", [P, LC], I32)
        last_t = sb("last_t", [P, LC], I32)
        last_f = sb("last_f", [P, LC])
        last_s = sb("last_s", [P, LC])
        mhalf = sb("mhalf", [P, 1])

        G = sb("G", [P, 2, CH, KVW])
        ef = sb("ef", [P, 2, CH, 4], I32)
        qs = sb("qs", [P, 2, ST, D])
        oh = sb("oh", [P, 2, CH, P])
        oht = sb("oht", [P, 2, 4, P])
        oh0 = sb("oh0", [P, 2])
        prod = sb("prod", [P, 2, 2, D])
        ev = sb("ev", [P, 2, 2, HV])
        acc = sb("acc", [P, 2, ST, HV])
        accr = sb("accr", [P, HV])
        dloc = sb("dloc", [P, 2, CH])
        samec = sb("samec", [P, 2, ST])
        lk = sb("lk", [P, 2, CH])
        msk = sb("msk", [P, 3, CH])
        bm = sb("bm", [P, CH])
        arep = sb("arep", [P, P])
        ats = sb("ats", [P, P + 1])
        sred = sb("sred", [P, P])
        S = sb("S", [P, P])
        scan1 = sb("scan1", [P, P])
        scan2 = sb("scan2", [P, P])
        v4 = sb("v4", [P, 2])
        rowS = sb("rowS", [1, 4, P])
        d0f = sb("d0f", [1, P])
        d1f = sb("d1f", [1, P])
        d0b = sb("d0b", [1, P])
        d1b = sb("d1b", [1, P])
        inr = sb("inr", [1, P])
        outr = sb("outr", [1, P])
        carry = sb("carry", [1, H])
        ct = sb("ct", [1, 5, H])
        rexp = sb("rexp", [1, H])
        cols = sb("cols", [P, 2])
        rt = sb("rt", [P, H])
        rm = sb("rm", [P, 2, H])
        df = sb("df", [P, P])
        ex = sb("ex", [P, 2, P])

        bank = [ctx.enter_context(nc.psum_tensor(f"bank{i}", [P, 512], F32)) for i in range(8)]

        Gf = G[:, :, :, :].rearrange("p a c w -> p (a c w)")
        used = [0]

        def carve(n):
            a = used[0]
            used[0] += n
            assert used[0] <= 2 * CH * KVW
            return Gf[:, a:a + n]

        st = sb("st", [P, 4, 6])
        mv = sb("mv", [P, 4, 2])
        vr = sb("vr", [P, 8])

        w_v = carve(2 * D).rearrange("p (k n) -> p k n", k=2)
        w_kq = carve(4 * D).rearrange("p (k n) -> p k n", k=2)
        xts, hts, hTs, kvos, qos, qns = [[carve(w) for _ in range(2)] for w in (D, D, D, KVW, D, D)]

        used[0] = 0
        w_p = carve(2 * D).rearrange("p (k n) -> p k n", k=2)
        w_1 = carve(2 * FFN).rearrange("p (k n) -> p k n", k=2)
        w_2 = carve(FC * D).rearrange("p (k n) -> p k n", k=FC)
        w_l = carve(2 * D).rearrange("p (k n) -> p k n", k=2)
        w_g = carve(2 * D).rearrange("p (k n) -> p k n", k=2)
        v_bp, v_g1, v_b1n, v_g2, v_b2n, v_b2, v_bl, v_al, v_ar = [carve(D) for _ in range(9)]
        v_b1 = carve(FC)
        xt, ht = carve(D), carve(D)
        at_in, at, atT, den = carve(HV), carve(D), carve(D), carve(2 * H)
        y, h1, h1T, gT = carve(D), carve(D), carve(D), carve(FFN)
        z, z2, xm, h2, h2T, hl, hlT, xh = [carve(D) for _ in range(8)]
        fo, tmpel, ero = carve(FTW), carve(D), carve(H)

        used[0] = 0
        v_gb = carve(D)
        fin_in, fin_xh, fin_a, fin_o, fin_d = [[carve(w) for _ in range(2)] for w in (HV, D, D, D, 2 * H)]

        ohf = oh[:, :, :, :].rearrange("p a c n -> p (a c n)")
        qsf = qs[:, :, :, :].rearrange("p a s n -> p (a s n)")
        cmp_ = [(ohf if c < 4 else qsf)[:, (c % 4) * NS:(c % 4 + 1) * NS] for c in range(LC)]
        cmpe = [ev[:, :, :, :].rearrange("p a k n -> p (a k n)")[:, c * NT:(c + 1) * NT] for c in range(LC)]
        S_ = {}
        for name in """const_made gather_free stats_made setup_loaded path_dve path_pe w_loaded
            q_x0 q_x1 q_dve q_rstd q_relu q_tr q_hT q_mm q_ka q_st0 q_st1 q_vq
            m_w m_acc m_h m_x m_dve0 m_dve1 m_dve2 m_dve3 m_dve4 m_var1 m_var2 m_var3 m_rs1 m_rs2 m_rs3
            m_tr0 m_tr1 m_tr2 m_tr3 m_cp0 m_cp1 m_cp2 m_cp3 m_mm0 m_mm1 m_mm2 m_mm3 m_w1 m_gelu
            m_sxh m_sft m_rdacc m_rdx f_acc0 f_acc1 f_xh0 f_xh1 f_dve f_st0 f_st1""".split():
            S_[name] = sem(name)
        L_ = []
        for layer in range(2):
            d = {}
            for name in """fld arep_made oh_made pat ats_made oht_tr oht_cp qexp prodd redd smade
                s_tr soft v4_made oh0_made rows_mm rows_cp row rowsdone cols_mm cols_cp r_exp bm_made
                m_made m_tr dmade ex_made ev_made agg accd resc init""".split():
                d[name] = sem(f"{name}_{layer}")
            d["efl"] = [sem(f"efl{layer}{p}") for p in range(2)]
            d["acs"] = [sem(f"acs{layer}{p}") for p in range(2)]
            d["gat"] = [[sem(f"gat{p}_{s}") for s in range(ST)] for p in range(2)] if layer == 0 else L_[0]["gat"]
            L_.append(d)

        FLD, SOFT, ROW = 7, 6, 13
        M0, M1, M2 = 2, 7, 11
        QN = 3
        FIN = 6
        block = ctx.enter_context(nc.Block())

        def hc(ap):
            return ap.rearrange("p (h c) -> p h c", h=H)

        def hv(ap):
            return ap.rearrange("p (h w) -> p h w", h=H)

        @block.sync
        def _(sp):
            sp.dma_start(last_i[:, :], last.rearrange("(p c) -> p c", c=LC)).then_inc(S_["setup_loaded"], 16)
            for w, src in ((w_v, Wv), (w_kq[:, :, 0:D], Wk), (w_kq[:, :, D:2 * D], Wq)):
                sp.dma_start(w, src.rearrange("(k p) n -> p k n", p=P)).then_inc(S_["w_loaded"], 16)

            def q_load(t, par):
                wait(sp, S_["q_dve"], QN * (t - 1))
                sp.dma_start(xts[par], x[bass.ds(t * P, P), :]).then_inc(S_[f"q_x{par}"], 16)

            def q_store(t, par):
                done = S_[f"q_st{par}"]
                sp.wait_ge(S_["q_relu"], t + 1)
                sp.dma_start(h_tab[bass.ds(t * P, P), :], hts[par]).then_inc(done, 16)
                sp.wait_ge(S_["q_vq"], t + 1)
                sp.wait_ge(S_["q_ka"], 2 * t + 2)
                sp.dma_start(kv_tab[bass.ds(t * P, P), :], kvos[par]).then_inc(done, 16)
                sp.dma_start(q_tab[bass.ds(t * P, P), :], qos[par]).then_inc(done, 16)

            q_load(0, 0)
            q_load(1, 1)
            with sp.Fori(0, NT // 2 - 1) as i:
                for par in range(2):
                    q_load(2 * i + par + 2, par)
                    q_store(2 * i + par, par)
            for par in range(2):
                q_store(NT - 2 + par, par)
            for par in range(2):
                sp.wait_ge(S_[f"q_st{par}"], 48 * (NT // 2))
            sp.wait_ge(S_["path_dve"], 1)

            def edge_loads(L, layer, b, par, i):
                wait(sp, L["smade"], b - 1)
                for s in range(ST):
                    t = sp.value_load(tile_row[0:1, bass.ds(b * ST + s, 1)], min_val=0, max_val=NT - 1)
                    m = nc.s_assert_within(sp.snap(b * ST + s - t), 0, NSPAN,
                                           skip_runtime_bounds_check_because="step = span + tile")
                    sp.dma_start(ef[:, par, 2 * s:2 * s + 2, :],
                                 edges[bass.ds(m * P, P), :].rearrange("p (k f) -> p k f", f=4)
                                 ).then_inc(L["efl"][par], 16)
                    if layer == 0:
                        sp.dma_start(qs[:, par, s, :], q_tab[bass.ds(t * P, P), :]).then_inc(L["efl"][par], 16)
                    else:
                        sp.dma_start(qs[:, par, s, 0:H], er_tab[bass.ds(t * P, P), :]).then_inc(L["efl"][par], 16)

            def sum_stores(L, b, par):
                for s in range(ST):
                    sp.wait_ge(L["accd"], b * ST + s + 1)
                    sp.dma_start(sums[bass.ds((b * ST + s) * P, P), :], acc[:, par, s, :]).then_inc(L["acs"][par], 16)

            def edge_phase(layer):
                L = L_[layer]
                for b in range(2):
                    edge_loads(L, layer, b, b, 0)
                with sp.Fori(1, NB // 2) as i:
                    for par in range(2):
                        edge_loads(L, layer, 2 * i + par, par, i)
                        sum_stores(L, 2 * i + par - 2, par)
                for b in (NB - 2, NB - 1):
                    sum_stores(L, b, b % 2)
                for par in range(2):
                    sp.wait_ge(L["acs"][par], 16 * ST * (NB // 2))

            edge_phase(0)

            for w, src in ((w_p, Wp), (w_1, W1), (w_2, W2), (w_l, Wl), (w_g, Wg)):
                sp.dma_start(w, src.rearrange("(k p) n -> p k n", p=P)).then_inc(S_["m_w"], 16)
            for v, src in ((v_bp, bp), (v_g1, g1), (v_b1n, b1n), (v_g2, g2), (v_b2n, b2n), (v_b2, b2),
                           (v_bl, bl), (v_al, al), (v_ar, ar)):
                sp.dma_start(v, src.partition_broadcast(P)).then_inc(S_["m_w"], 16)
            sp.dma_start(v_b1, b1.rearrange("(c p) -> p c", p=P), allow_slow_non_contiguous=True).then_inc(S_["m_w"], 16)

            def m_turn(t):
                if not isinstance(t, int) or t < NT:
                    wait(sp, S_["m_rdacc"], t)
                    e = sp.value_load(endstep[0:1, bass.ds(t, 1)], min_val=0, max_val=NS - 1)
                    sp.dma_start(at_in, sums[bass.ds(e * P, P), :]).then_inc(S_["m_acc"], 16)
                if not isinstance(t, int) or 1 <= t <= NT:
                    wait(sp, S_["m_var1"], t - 1)
                    sp.dma_start(ht, h_tab[bass.ds((t - 1) * P, P), :]).then_inc(S_["m_h"], 16)
                if not isinstance(t, int) or 2 <= t <= NT + 1:
                    wait(sp, S_["m_rdx"], t - 2)
                    sp.dma_start(xt, x[bass.ds((t - 2) * P, P), :]).then_inc(S_["m_x"], 16)
                if not isinstance(t, int) or 3 <= t <= NT + 2:
                    u = t - 3
                    sp.wait_ge(S_["m_dve3"], 2 * u + 2)
                    sp.dma_start(xh_tab[bass.ds(u * P, P), :], xh).then_inc(S_["m_sxh"], 16)
                if not isinstance(t, int) or t >= 4:
                    u = t - 4
                    sp.wait_ge(S_["m_dve4"], 5 * u + 5)
                    sp.dma_start(ft_tab[bass.ds(u * P, P), :], fo).then_inc(S_["m_sft"], 16)
                    sp.dma_start(er_tab[bass.ds(u * P, P), :], ero).then_inc(S_["m_sft"], 16)

            for t in range(4):
                m_turn(t)
            with sp.Fori(4, NT) as t:
                m_turn(t)
            for t in range(NT, NT + 4):
                m_turn(t)
            sp.wait_ge(S_["m_sxh"], 16 * NT)
            sp.wait_ge(S_["m_sft"], 32 * NT)

            edge_phase(1)

            sp.dma_start(v_gb, gb.partition_broadcast(P)).then_inc(S_["m_w"], 16)

            def f_load(t, par, i):
                wait(sp, S_["f_dve"], FIN * (t - 1))
                e = sp.value_load(endstep[0:1, bass.ds(t, 1)], min_val=0, max_val=NS - 1)
                sp.dma_start(fin_in[par], sums[bass.ds(e * P, P), :]).then_inc(S_[f"f_acc{par}"], 16)
                sp.dma_start(fin_xh[par], xh_tab[bass.ds(t * P, P), :]).then_inc(S_[f"f_xh{par}"], 16)

            def f_store(t, par, rows):
                sp.wait_ge(S_["f_dve"], FIN * (t + 1))
                sp.dma_start(out[bass.ds(t * P, rows), :], fin_o[par][0:rows, :]).then_inc(S_[f"f_st{par}"], 16)

            f_load(0, 0, 0)
            f_load(1, 1, 0)
            with sp.Fori(0, NT // 2 - 1) as i:
                for par in range(2):
                    f_load(2 * i + par + 2, par, i)
                    f_store(2 * i + par, par, P)
            f_store(NT - 2, 0, P)
            f_store(NT - 1, 1, N - (NT - 1) * P)
            for par in range(2):
                sp.wait_ge(S_[f"f_st{par}"], 16 * (NT // 2))

        @block.gpsimd
        def _(pool):
            cm = S_["const_made"]
            pool.memset(ident[:, :], 0.0).then_inc(cm, 1)
            pool.memset(ones[:, :], 1.0).then_inc(cm, 1)
            pool.memset(mhalf[:, :], -0.5).then_inc(cm, 1)
            pool.wait_ge(cm, 3)
            pool.affine_select(out=ident[:, :], in_=ident[:, :], compare_op=ALU.not_equal, fill=1.0,
                               base=0, pattern=[[-1, P]], channel_multiplier=1).then_inc(cm, 1)
            pool.iota(lane[:, :], [[1, P]], base=0, channel_multiplier=0,
                      allow_small_or_imprecise_dtypes=True).then_inc(cm, 1)
            pool.iota(steps[:, :], [[1, NS]], base=0, channel_multiplier=0,
                      allow_small_or_imprecise_dtypes=True).then_inc(cm, 1)
            pool.iota(spanid[:, :], [[1, LC]], base=0, channel_multiplier=LC,
                      allow_small_or_imprecise_dtypes=True).then_inc(cm, 1)

            def rstd(k, ready, n, done):
                pool.wait_ge(ready, n + 1)
                pool.tensor_tensor(vr[:, 2 * k + 1:2 * k + 2], vr[:, 2 * k:2 * k + 1], mhalf[:, :],
                                   ALU.pow).then_inc(done, 1)

            pool.wait_ge(cm, 7)
            with pool.Fori(0, NT) as t:
                rstd(0, S_["q_rstd"], 2 * t, S_["q_rstd"])

            def gathers(L, layer, b, par, i):
                pool.wait_ge(L["efl"][par], 32 * ST * (i + 1))
                for c in range(CH):
                    wait(pool, L["ev_made"], (b - 2) * ST + c // 2 + 1)
                    pool.sem_inc(S_["gather_free"], 1)
                    tab, w = (kv_tab, KVW) if layer == 0 else (ft_tab, FTW)
                    pool.indirect_dma_start(
                        out=G[:, par, c, 0:w], out_offset=None, in_=tab,
                        in_offset=bass.IndirectOffsetOnAxis(ap=ef[:, par, c, 0:1], axis=0),
                    ).then_inc(L["gat"][par][c // 2], 16)

            def edge_phase(layer):
                L = L_[layer]
                for b in range(2):
                    gathers(L, layer, b, b, 0)
                with pool.Fori(1, NB // 2) as i:
                    for par in range(2):
                        gathers(L, layer, 2 * i + par, par, i)

            edge_phase(0)

            for t in range(4):
                for k in (2, 3, 1):
                    first = 1 if k == 1 else 2
                    if first <= t:
                        rstd(k, S_[f"m_var{k}"], t - first, S_[f"m_rs{k}"])
            with pool.Fori(4, NT) as t:
                for k in (2, 3, 1):
                    rstd(k, S_[f"m_var{k}"], t - (1 if k == 1 else 2), S_[f"m_rs{k}"])
            for t in range(NT, NT + 2):
                for k in (2, 3, 1):
                    first = 1 if k == 1 else 2
                    if t < NT + first:
                        rstd(k, S_[f"m_var{k}"], t - first, S_[f"m_rs{k}"])
            edge_phase(1)

        @block.scalar
        def _(act):
            def copy(o, i_, s):
                act.activation(o, i_, ACT.Copy).then_inc(s, 1)

            act.wait_ge(S_["const_made"], 7)

            def q_turn(t, par, i):
                if not isinstance(t, int) or t < NT:
                    act.wait_ge(S_["q_dve"], QN * (t + 1))
                    wait(act, S_[f"q_st{par}"], 48 * i)
                    act.activation(hts[par], qns[par], ACT.Relu).then_inc(S_["q_relu"], 1)
                    act.wait_ge(S_["q_tr"], t + 1)
                    wait(act, S_["q_mm"], t - 1)
                    copy(hTs[par], bank[par][:, 0:D], S_["q_hT"])
                if not isinstance(t, int) or t > 0:
                    act.wait_ge(S_["q_mm"], t)
                    q, qi = 1 - par, (i if par else i - 1)
                    wait(act, S_[f"q_st{q}"], 48 * qi)
                    copy(kvos[q][:, 0:D], bank[2 + q][:, 0:D], S_["q_ka"])
                    copy(qos[q], bank[2 + q][:, D:2 * D], S_["q_ka"])

            def q_turns(turn, eng):
                turn(0, 0, 0)
                turn(1, 1, 0)
                with eng.Fori(1, NT // 2) as i:
                    for par in range(2):
                        turn(2 * i + par, par, i)
                turn(NT, 0, NT // 2)

            q_turns(q_turn, act)

            def edge_a(L, b, par):
                act.wait_ge(L["pat"], b + 1)
                wait(act, L["soft"], SOFT * b)
                copy(ats[:, 0:P], bank[7][:, 0:P], L["ats_made"])
                for g in range(4):
                    act.wait_ge(L["oht_tr"], b * 4 + g + 1)
                    wait(act, L["qexp"], b * ST + 2 * g - 2)
                    if g == 2:
                        act.wait_ge(L["oh0_made"], b + 1)
                    copy(oht[:, g % 2, :, :].rearrange("p c n -> p (c n)"), bank[g % 2][:, :], L["oht_cp"])
                    if g == 0:
                        act.wait_ge(L["oht_cp"], b * 4 + 1)
                        copy(oh0[:, par:par + 1], oht[:, 0, 0, 0:1], L["oh0_made"])

            def edge_b(L, b, par):
                act.wait_ge(L["rows_mm"], b + 1)
                copy(rowS[:, :, :].rearrange("p q n -> p (q n)"), bank[7][0:1, :], L["rows_cp"])
                act.wait_ge(L["row"], ROW * b + ROW)
                act.activation(rexp[:, :], ct[:, 4, :], ACT.Exp).then_inc(L["r_exp"], 1)
                act.wait_ge(L["cols_mm"], b + 1)
                copy(cols[:, :], bank[7][:, 0:2], L["cols_cp"])
                act.wait_ge(L["dmade"], b + 1)
                act.activation(ex[:, par, :], df[:, :], ACT.Exp).then_inc(L["ex_made"], 1)

            def edge_phase(layer):
                L = L_[layer]
                for b in range(2):
                    edge_a(L, b, b)
                    edge_b(L, b, b)
                with act.Fori(1, NB // 2) as i:
                    for par in range(2):
                        edge_a(L, 2 * i + par, par)
                        edge_b(L, 2 * i + par, par)

            edge_phase(0)

            act.wait_ge(S_["m_w"], 16 * 15)

            def m_turn(t):
                def on(k):
                    return not isinstance(t, int) or k <= t < NT + k
                for k, dst, b in ((3, hlT, 5), (2, h2T, 4)):
                    if on(k):
                        act.wait_ge(S_[f"m_tr{k}"], t - k + 1)
                        copy(dst, bank[b][:, 0:D], S_[f"m_cp{k}"])
                if on(1):
                    u = t - 1
                    act.wait_ge(S_["m_tr1"], u + 1)
                    copy(h1T, bank[1][:, 0:D], S_["m_cp1"])
                    for f in range(FC):
                        if f % 4 == 0:
                            act.wait_ge(S_["m_w1"], 2 * u + f // 4 + 1)
                        act.activation(gT[:, f * P:(f + 1) * P], bank[2 + f // 4][:, (f % 4) * P:(f % 4 + 1) * P],
                                       ACT.Gelu, bias=v_b1[:, f:f + 1]).then_inc(S_["m_gelu"], 1)
                if on(0):
                    act.wait_ge(S_["m_tr0"], t + 1)
                    copy(atT, bank[0][:, 0:D], S_["m_cp0"])

            for t in range(4):
                m_turn(t)
            with act.Fori(4, NT) as t:
                m_turn(t)
            for t in range(NT, NT + 4):
                m_turn(t)

            edge_phase(1)

        @block.tensor
        def _(pe):
            def mm(o, a, r, first=True, end=True):
                return nc.tensor.matmul(o, a, r, start=first, stop=end)

            def tr(o, i_):
                return nc.tensor.transpose(o, i_, ident[:, :])

            pe.wait_ge(S_["const_made"], 7)
            pe.wait_ge(S_["path_pe"], 2 * LC)
            half = NS // 2
            for c in range(LC):
                for k in range(2):
                    mm(bank[4 + k][:, 0:half], ones[:, :], cmp_[c][:, k * half:(k + 1) * half],
                       c == 0, c == LC - 1)
                m = mm(bank[6][:, 0:NT], ones[:, :], cmpe[c], c == 0, c == LC - 1)
            m.then_inc(S_["path_pe"], 1)

            pe.wait_ge(S_["w_loaded"], 48)

            def q_turn(t, par, i):
                if not isinstance(t, int) or t < NT:
                    pe.wait_ge(S_["q_relu"], t + 1)
                    wait(pe, S_["q_hT"], t - 1)
                    tr(bank[par][:, 0:P], hts[par][:, 0:P])
                    tr(bank[par][:, P:D], hts[par][:, P:D]).then_inc(S_["q_tr"], 1)
                if not isinstance(t, int) or t > 0:
                    q = 1 - par
                    pe.wait_ge(S_["q_hT"], t)
                    wait(pe, S_["q_vq"], t - 2)
                    wait(pe, S_["q_ka"], 2 * (t - 2))
                    for k in range(2):
                        mm(bank[2 + q][:, :], hTs[q][:, k * P:(k + 1) * P], w_kq[:, k, :], k == 0, k == 1)
                    for k in range(2):
                        m = mm(bank[4 + q][:, 0:D], hTs[q][:, k * P:(k + 1) * P], w_v[:, k, :], k == 0, k == 1)
                    m.then_inc(S_["q_mm"], 1)

            q_turn(0, 0, 0)
            q_turn(1, 1, 0)
            with pe.Fori(1, NT // 2) as i:
                for par in range(2):
                    q_turn(2 * i + par, par, i)
            q_turn(NT, 0, NT // 2)

            def edge_a(L, layer, b, par, i):
                pe.wait_ge(L["arep_made"], b + 1)
                wait(pe, L["ats_made"], b)
                tr(bank[7][:, 0:P], arep[:, :]).then_inc(L["pat"], 1)
                pe.wait_ge(L["efl"][par], 32 * ST * (i + 1))
                for g in range(5):
                    if g < 4:
                        pe.wait_ge(L["oh_made"], b * CH + 4 * g + 4)
                        wait(pe, L["oht_cp"], b * 4 + g - 1)
                        for k in range(4):
                            m = tr(bank[g % 2][:, k * P:(k + 1) * P], oh[:, par, 4 * g + k, :])
                        m.then_inc(L["oht_tr"], 1)
                    if g >= 1:
                        e = g - 1
                        pe.wait_ge(L["oht_cp"], b * 4 + e + 1)
                        for s in (2 * e, 2 * e + 1):
                            if layer == 0:
                                wait(pe, L["prodd"], b * ST + s - 1)
                            elif s == 0:
                                wait(pe, L["smade"], b - 1)
                            for k in range(2):
                                a = oht[:, e % 2, 2 * (s % 2) + k, :]
                                if layer == 0:
                                    m = mm(bank[2 + s % 2][:, k * D:(k + 1) * D], a, qs[:, par, s, :])
                                else:
                                    c = 2 * s + k
                                    m = mm(bank[2 + par][:, c * H:(c + 1) * H], a, qs[:, par, s, 0:H])
                            m.then_inc(L["qexp"], 1)

            def agg(L, b, par, s):
                pe.wait_ge(L["ev_made"], b * ST + s + 1)
                wait(pe, L["accd"], b * ST + s - 1)
                o = bank[4 + s % 2][:, 0:HV]
                mm(o, oh[:, par, 2 * s, :], ev[:, s % 2, 0, :], True, False)
                mm(o, oh[:, par, 2 * s + 1, :], ev[:, s % 2, 1, :], False, True).then_inc(L["agg"], 1)

            def edge_b(L, b, par):
                prev = b - 1
                do = not (isinstance(b, int) and b == 0)

                def aggs(*ss):
                    if do:
                        for s in ss:
                            agg(L, prev, 1 - par, s)

                pe.wait_ge(L["smade"], b + 1)
                tr(bank[6][:, 0:P], S[:, :]).then_inc(L["s_tr"], 1)
                aggs(0)
                pe.wait_ge(L["v4_made"], 2 * b + 2)
                pe.wait_ge(L["soft"], SOFT * b + 2)
                for q, v in enumerate((scan1[:, P - 1:P], scan2[:, 0:1], v4[:, 0:1], v4[:, 1:2])):
                    m = mm(bank[7][0:1, q * P:(q + 1) * P], v, ident[:, :])
                m.then_inc(L["rows_mm"], 1)
                aggs(1, 2)
                pe.wait_ge(L["row"], ROW * b + ROW)
                pe.wait_ge(L["r_exp"], b + 1)
                mm(bank[7][:, 0:1], inr[0:1, :], ones[0:1, 0:1])
                mm(bank[7][:, 1:2], outr[0:1, :], ones[0:1, 0:1])
                mm(bank[7][:, 8:8 + H], ones[0:1, :], rexp[0:1, :]).then_inc(L["cols_mm"], 1)
                aggs(3)
                pe.wait_ge(L["soft"], SOFT * b + 4)
                tr(bank[6][:, P:2 * P], scan2[:, :]).then_inc(L["m_tr"], 1)
                aggs(4, 5, 6, 7)

            def edge_phase(layer):
                L = L_[layer]
                for b in range(2):
                    edge_a(L, layer, b, b, 0)
                    edge_b(L, b, b)
                with pe.Fori(1, NB // 2) as i:
                    for par in range(2):
                        edge_a(L, layer, 2 * i + par, par, i)
                        edge_b(L, 2 * i + par, par)
                for s in range(ST):
                    agg(L, NB - 1, 1, s)

            edge_phase(0)
            pe.wait_ge(S_["m_w"], 16 * 15)

            def m_turn(t):
                def on(k):
                    return not isinstance(t, int) or k <= t < NT + k

                def stage(k, src, dst, b, w, ready, count):
                    pe.wait_ge(ready, count)
                    tr(bank[b][:, 0:P], src[:, 0:P])
                    tr(bank[b][:, P:D], src[:, P:D]).then_inc(S_[f"m_tr{k}"], 1)
                    pe.wait_ge(S_[f"m_cp{k}"], t - k + 1)
                    if w is not None:
                        for c in range(2):
                            m = mm(bank[b][:, D:2 * D], dst[:, c * P:(c + 1) * P], w[:, c, :], c == 0, c == 1)
                        m.then_inc(S_[f"m_mm{k}"], 1)

                if on(3):
                    stage(3, hl, hlT, 5, w_g, S_["m_dve3"], 2 * (t - 3) + 2)
                if on(2):
                    stage(2, h2, h2T, 4, w_l, S_["m_dve2"], M2 * (t - 2) + M2)
                if on(1):
                    u = t - 1
                    stage(1, h1, h1T, 1, None, S_["m_dve1"], M1 * u + M1)
                    for f in range(FC):
                        for c in range(2):
                            m = mm(bank[2 + f // 4][:, (f % 4) * P:(f % 4 + 1) * P],
                                   w_1[:, c, f * P:(f + 1) * P], h1T[:, c * P:(c + 1) * P], c == 0, c == 1)
                        if f % 4 == 3:
                            m.then_inc(S_["m_w1"], 1)
                    for f in range(FC):
                        pe.wait_ge(S_["m_gelu"], FC * u + f + 1)
                        m = mm(bank[1][:, D:2 * D], gT[:, f * P:(f + 1) * P], w_2[:, f, :], f == 0, f == FC - 1)
                    m.then_inc(S_["m_mm1"], 1)
                if on(0):
                    stage(0, at, atT, 0, w_p, S_["m_rdacc"], t + 1)

            for t in range(4):
                m_turn(t)
            with pe.Fori(4, NT) as t:
                m_turn(t)
            for t in range(NT, NT + 4):
                m_turn(t)
            edge_phase(1)

        @block.vector
        def _(dve):
            V = nc.vector
            dve.wait_ge(S_["const_made"], 7)
            dve.wait_ge(S_["setup_loaded"], 16)
            c0 = Chain(dve, L_[0]["init"], 99)
            c0.start(0)
            c0.did(V.memset(ats[:, P:P + 1], 0.0))
            c0.did(V.memset(d0f[:, :], -BIG))
            c0.did(V.memset(d0b[:, :], -BIG))
            c0.did(V.memset(d1b[:, :], -BIG))
            c0.did(V.memset(carry[:, :], -BIG))
            c0.did(V.memset(acc[:, 1, ST - 1, :], 0.0))
            for kvo in kvos:
                c0.did(V.memset(kvo[:, D:KVW], 1.0))
            c0.seq(V.tensor_scalar(last_t[:, :], last_i[:, :], 7, None, ALU.logical_shift_right))
            c0.seq(V.tensor_copy(last_f[:, :], last_t[:, :]))
            c0.seq(V.tensor_tensor(last_s[:, :], last_f[:, :], spanid[:, :], ALU.add))
            for c in range(LC):
                V.tensor_scalar(cmp_[c], steps[:, :], last_s[:, c:c + 1], None,
                                ALU.is_gt).then_inc(S_["path_pe"], 1)
                V.tensor_scalar(cmpe[c], steps[:, 0:NT], last_f[:, c:c + 1], None,
                                ALU.is_ge).then_inc(S_["path_pe"], 1)
            dve.wait_ge(S_["path_pe"], 2 * LC + 1)
            half = NS // 2
            for k in range(2):
                c0.seq(V.tensor_tensor(tile_of[:, k * half:(k + 1) * half], steps[:, k * half:(k + 1) * half],
                                       bank[4 + k][:, 0:half], ALU.subtract))
            c0.seq(V.memset(same[:, 0:1], 0.0))
            c0.seq(V.tensor_tensor(same[:, 1:NS], tile_of[:, 1:NS], tile_of[:, 0:NS - 1], ALU.is_equal))
            c0.seq(V.tensor_tensor(endf[:, :], bank[6][0:1, 0:NT], steps[0:1, 0:NT], ALU.add))
            c0.seq(V.tensor_copy(endstep[:, :], endf[:, :]))
            V.tensor_copy(tile_row[:, :], tile_of[0:1, :]).then_inc(S_["path_dve"], 1)

            cq = Chain(dve, S_["q_dve"], QN)

            def q_turn(t, par, i):
                if not isinstance(t, int) or t < NT:
                    cq.start(t)
                    dve.wait_ge(S_[f"q_x{par}"], 16 * (i + 1))
                    wait(dve, S_["q_relu"], t - 1)
                    cq.seq(V.bn_stats(st[:, 0, :], xts[par]))
                    dve.sem_inc(S_["stats_made"], 1)
                    cq.seq(V.bn_aggr(mv[:, 0, :], st[:, 0, :]))
                    V.tensor_scalar(vr[:, 0:1], mv[:, 0, 1:2], EPS, None, ALU.add).then_inc(S_["q_rstd"], 1)
                    dve.wait_ge(S_["q_rstd"], 2 * t + 2)
                    cq.did(V.tensor_scalar(qns[par], xts[par], mv[:, 0, 0:1], vr[:, 1:2],
                                           ALU.subtract, ALU.mult))
                    cq.end()
                if not isinstance(t, int) or t > 0:
                    q, qi = 1 - par, (i if par else i - 1)
                    dve.wait_ge(S_["q_mm"], t)
                    wait(dve, S_[f"q_st{q}"], 48 * qi)
                    V.tensor_copy(hv(kvos[q][:, D:KVW])[:, :, 0:HD],
                                  hv(bank[4 + q][:, 0:D])).then_inc(S_["q_vq"], 1)

            q_turn(0, 0, 0)
            q_turn(1, 1, 0)
            with dve.Fori(1, NT // 2) as i:
                for par in range(2):
                    q_turn(2 * i + par, par, i)
            q_turn(NT, 0, NT // 2)

            def fields(L, layer, b, par, i):
                ch = Chain(dve, L["fld"], FLD)
                ch.start(b)
                dve.wait_ge(L["efl"][par], 32 * ST * (i + 1))
                wait(dve, L["accd"], (b - 1) * ST)
                wait(dve, L["smade"], b)
                wait(dve, L["arep_made"], b)
                wait(dve, L["bm_made"], b)
                dst = ef[:, par, :, 1]
                ch.did(V.scalar_tensor_tensor(
                    dloc[:, par, :].rearrange("p (s k) -> p s k", k=2),
                    tile_of[:, bass.ds(b * ST, ST)].unsqueeze(2).to_broadcast([P, ST, 2]), -float(P),
                    dst.rearrange("p (s k) -> p s k", k=2), ALU.mult, ALU.add))
                ch.did(V.tensor_copy(samec[:, par, :], same[:, bass.ds(b * ST, ST)]))
                ch.seq(V.tensor_tensor(lk[:, 0, :], dst, ef[:, par, :, 2], ALU.is_equal))
                ch.did(V.tensor_scalar(msk[:, 0, :], dloc[:, par, :], 0.0, BIG, ALU.is_ge, ALU.mult))
                ch.did(V.tensor_scalar(msk[:, 1, :], dloc[:, par, :], float(P), BIG, ALU.is_lt, ALU.mult))
                ch.seq(V.tensor_scalar(lk[:, 1, :], lk[:, 0, :], -1.0, BIG, ALU.add, ALU.mult))
                V.tensor_copy(hc(arep[:, :]), lk[:, 1, :].unsqueeze(1).to_broadcast([P, H, CH])
                              ).then_inc(L["arep_made"], 1)
                ch.seq(V.tensor_tensor(msk[:, 2, :], msk[:, 0, :], msk[:, 1, :], ALU.add))
                ch.end()
                if layer == 0:
                    V.scalar_tensor_tensor(bm[:, :], msk[:, 2, :], -2 * BIG, ef[:, par, :, 3].bitcast(F32),
                                           ALU.add, ALU.add).then_inc(L["bm_made"], 1)
                else:
                    V.tensor_scalar(bm[:, :], msk[:, 2, :], -2 * BIG, None, ALU.add).then_inc(L["bm_made"], 1)
                for c in range(CH):
                    V.tensor_scalar(oh[:, par, c, :], lane[:, :], dloc[:, par, c:c + 1], None,
                                    ALU.is_equal).then_inc(L["oh_made"], 1)

            def scores(L, layer, b, par, i):
                wait(dve, L["smade"], b)
                wait(dve, L["dmade"], b)
                if layer == 0:
                    def reduce(s):
                        dve.wait_ge(L["prodd"], b * ST + s + 1)
                        V.tensor_reduce(hc(sred[:, :])[:, :, 2 * s:2 * s + 2].rearrange("p h c -> p c h"),
                                        prod[:, s % 2, :, :].rearrange("p k (h w) -> p k h w", h=H), AXX,
                                        ALU.add).then_inc(L["redd"], 1)
                    for s in range(ST):
                        dve.wait_ge(L["gat"][par][s], 32 * (i + 1))
                        dve.wait_ge(L["qexp"], b * ST + s + 1)
                        wait(dve, L["redd"], b * ST + s - 1)
                        V.tensor_tensor(prod[:, s % 2, :, :], G[:, par, 2 * s:2 * s + 2, 0:D],
                                        bank[2 + s % 2][:, :].rearrange("p (k n) -> p k n", k=2),
                                        ALU.mult).then_inc(L["prodd"], 1)
                        if s:
                            reduce(s - 1)
                    reduce(ST - 1)
                    dve.wait_ge(L["redd"], b * ST + ST)
                    dve.wait_ge(L["bm_made"], b + 1)
                    V.scalar_tensor_tensor(hc(S[:, :]), hc(sred[:, :]), float(HD) ** -0.5,
                                           bm[:, :].unsqueeze(1).to_broadcast([P, H, CH]),
                                           ALU.mult, ALU.add).then_inc(L["smade"], 1)
                else:
                    for s in range(ST):
                        dve.wait_ge(L["gat"][par][s], 32 * (NB // 2 + i + 1))
                    dve.wait_ge(L["qexp"], b * ST + ST)
                    V.tensor_tensor(hc(sred[:, :]), G[:, par, :, HV:FTW].rearrange("p c h -> p h c"),
                                    bank[2 + par][:, 0:P].rearrange("p (c h) -> p h c", h=H),
                                    ALU.add).then_inc(L["redd"], 1)
                    dve.wait_ge(L["redd"], 2 * b + 1)
                    V.scalar_tensor_tensor(prod[:, 0, 0, 0:P], sred[:, :], 0.2, sred[:, :],
                                           ALU.mult, ALU.max).then_inc(L["redd"], 1)
                    dve.wait_ge(L["redd"], 2 * b + 2)
                    dve.wait_ge(L["bm_made"], b + 1)
                    V.tensor_tensor(hc(S[:, :]), hc(prod[:, 0, 0, 0:P]),
                                    bm[:, :].unsqueeze(1).to_broadcast([P, H, CH]),
                                    ALU.add).then_inc(L["smade"], 1)

            def weigh(L, layer, b, par, s):
                if s >= 2:
                    dve.wait_ge(L["agg"], b * ST + s - 1)
                val = G[:, par, 2 * s:2 * s + 2, D:KVW] if layer == 0 else G[:, par, 2 * s:2 * s + 2, 0:HV]
                V.tensor_tensor(ev[:, s % 2, :, :].rearrange("p k (h w) -> p k h w", h=H),
                                val.rearrange("p k (h w) -> p k h w", h=H),
                                hc(ex[:, par, :])[:, :, 2 * s:2 * s + 2].rearrange("p h k -> p k h")
                                .unsqueeze(3).to_broadcast([P, 2, H, HD + 1]),
                                ALU.mult).then_inc(L["ev_made"], 1)

            def add(L, b, par, s):
                dve.wait_ge(L["agg"], b * ST + s + 1)
                if s:
                    prev = acc[:, par, s - 1, :]
                    dve.wait_ge(L["accd"], b * ST + s)
                else:
                    prev = accr[:, :]
                    dve.wait_ge(L["resc"], b + 1)
                V.scalar_tensor_tensor(acc[:, par, s, :], prev, samec[:, par, s:s + 1], bank[4 + s % 2][:, 0:HV],
                                       ALU.mult, ALU.add).then_inc(L["accd"], 1)

            def begin(L, b, par, i):
                dve.wait_ge(L["ex_made"], b + 1)
                wait(dve, L["accd"], b * ST)
                wait(dve, L["acs"][par], 16 * ST * i)
                V.tensor_tensor(hv(accr[:, :]), hv(acc[:, 1 - par, ST - 1, :]),
                                rm[:, par, :].unsqueeze(2).to_broadcast([P, H, HD + 1]),
                                ALU.mult).then_inc(L["resc"], 1)

            def turn(L, layer, b, par, i, more):
                scores(L, layer, b, par, i)
                q, pi = 1 - par, (i if par else i - 1)
                do = not (isinstance(b, int) and b == 0)

                def w(*cs):
                    if do:
                        for c in cs:
                            weigh(L, layer, b - 1, q, c)

                def a(*ss):
                    if do:
                        for s in ss:
                            add(L, b - 1, q, s)

                if do:
                    begin(L, b - 1, q, pi)
                w(0)
                ch = Chain(dve, L["soft"], SOFT)
                ch.start(b)
                dve.wait_ge(L["s_tr"], b + 1)
                dve.wait_ge(L["ats_made"], b + 1)
                wait(dve, L["soft"], SOFT * b)
                ST_ = bank[6][:, 0:P]
                ch.did(V.tensor_tensor_scan(scan1[:, :], ats[:, 0:P], ST_, -BIG, ALU.add, ALU.max))
                ch.did(V.tensor_tensor_scan(scan2[:, P - 1::-1], ats[:, P:0:-1], ST_[:, P - 1::-1], -BIG,
                                            ALU.add, ALU.max))
                V.tensor_reduce(v4[:, 0:1], ats[:, 1:P], AXX, ALU.min).then_inc(L["v4_made"], 1)
                V.tensor_copy(v4[:, 1:2], ats[:, 0:1]).then_inc(L["v4_made"], 1)
                w(1)
                a(0)
                w(2)
                r = Chain(dve, L["row"], ROW)
                r.start(b)
                dve.wait_ge(L["rows_cp"], b + 1)
                wait(dve, L["row"], ROW * b)
                l_, f_, w_, a_ = [hc(rowS[:, k, :]) for k in range(4)]
                r.did(V.tensor_tensor(hc(d0f[:, :])[:, :, 1:], w_[:, :, :CH - 1], a_[:, :, 1:], ALU.add))
                r.did(V.tensor_tensor(hc(d1f[:, :])[:, :, 1:], l_[:, :, :CH - 1], a_[:, :, 1:], ALU.add))
                r.did(V.tensor_tensor(hc(d1f[:, :])[:, :, 0], carry[:, :], a_[:, :, 0], ALU.add))
                r.did(V.tensor_tensor(hc(d0b[:, :])[:, :, :CH - 1], w_[:, :, 1:], a_[:, :, 1:], ALU.add))
                r.seq(V.tensor_tensor(hc(d1b[:, :])[:, :, :CH - 1], f_[:, :, 1:], a_[:, :, 1:], ALU.add))
                r.did(V.tensor_tensor_scan(inr[:, :], d0f[:, :], d1f[:, :], -BIG, ALU.add, ALU.max))
                r.seq(V.tensor_tensor_scan(outr[:, P - 1::-1], d0b[:, P - 1::-1], d1b[:, P - 1::-1], -BIG,
                                           ALU.add, ALU.max))
                r.did(V.tensor_tensor(ct[:, 0, :], w_[:, :, CH - 1], hc(inr[:, :])[:, :, CH - 1], ALU.add))
                r.seq(V.tensor_tensor(ct[:, 1, :], w_[:, :, 0], hc(outr[:, :])[:, :, 0], ALU.add))
                r.did(V.tensor_tensor(carry[:, :], ct[:, 0, :], l_[:, :, CH - 1], ALU.max))
                r.seq(V.tensor_tensor(ct[:, 2, :], ct[:, 1, :], f_[:, :, 0], ALU.max))
                r.seq(V.tensor_tensor(ct[:, 3, :], ct[:, 2, :], hc(inr[:, :])[:, :, 0], ALU.max))
                r.did(V.tensor_tensor(ct[:, 4, :], hc(d1f[:, :])[:, :, 0], ct[:, 3, :], ALU.subtract))
                r.end()
                a(1)
                w(3)
                a(2)
                dve.wait_ge(L["cols_cp"], b + 1)
                ch.seq(V.tensor_tensor_scan(scan1[:, :], ats[:, 0:P], ST_, cols[:, 0:1], ALU.add, ALU.max))
                ch.did(V.tensor_tensor_scan(scan2[:, P - 1::-1], ats[:, P:0:-1], scan1[:, P - 1::-1],
                                            cols[:, 1:2], ALU.add, ALU.max))
                dve.wait_ge(L["oh0_made"], b + 1)
                ch.seq(V.tensor_scalar(rt[:, :], bank[7][:, 8:8 + H], -1.0, oh0[:, par:par + 1], ALU.add, ALU.mult))
                ch.seq(V.tensor_scalar(rm[:, par, :], rt[:, :], 1.0, None, ALU.add))
                ch.end()
                w(4)
                a(3)
                dve.wait_ge(L["m_tr"], b + 1)
                V.tensor_tensor(df[:, :], S[:, :], bank[6][:, P:2 * P], ALU.subtract).then_inc(L["dmade"], 1)
                w(5)
                a(4)
                w(6)
                a(5)
                w(7)
                a(6, 7)
                if more:
                    fields(L, layer, b + 1, q, i + 1 if par else i)

            def edge_phase(layer):
                L = L_[layer]
                fields(L, layer, 0, 0, 0)
                turn(L, layer, 0, 0, 0, True)
                turn(L, layer, 1, 1, 0, True)
                with dve.Fori(1, NB // 2 - 1) as i:
                    for par in range(2):
                        turn(L, layer, 2 * i + par, par, i, True)
                turn(L, layer, NB - 2, 0, NB // 2 - 1, True)
                turn(L, layer, NB - 1, 1, NB // 2 - 1, False)
                begin(L, NB - 1, 1, NB // 2 - 1)
                for s in range(ST):
                    weigh(L, layer, NB - 1, 1, s)
                    if s:
                        add(L, NB - 1, 1, s - 1)
                add(L, NB - 1, 1, ST - 1)

            edge_phase(0)

            dve.wait_ge(S_["m_w"], 16 * 15)
            c1 = Chain(dve, L_[1]["init"], 99)
            c1.start(0)
            c1.did(V.memset(carry[:, :], -BIG))
            c1.did(V.memset(fo[:, 0:HV], 1.0))
            c1.sync()
            first_acc = V.memset(acc[:, 1, ST - 1, :], 0.0)
            c1.seq(first_acc)

            def norm(ch, k, src, dst, var, rs, n):
                ch.seq(V.bn_stats(st[:, k, :], src))
                dve.sem_inc(S_["stats_made"], 1)
                ch.seq(V.bn_aggr(mv[:, k, :], st[:, k, :]))
                V.tensor_scalar(vr[:, 2 * k:2 * k + 1], mv[:, k, 1:2], EPS, None, ALU.add).then_inc(var, 1)
                dve.wait_ge(rs, n + 1)
                ch.seq(V.tensor_scalar(dst, src, mv[:, k, 0:1], vr[:, 2 * k + 1:2 * k + 2],
                                       ALU.subtract, ALU.mult))

            def m_turn(t):
                def on(k):
                    return not isinstance(t, int) or k <= t < NT + k
                if on(4):
                    u = t - 4
                    ch = Chain(dve, S_["m_dve4"], 5)
                    ch.start(u)
                    dve.wait_ge(S_["m_mm3"], u + 1)
                    wait(dve, S_["m_sft"], 32 * u)
                    feat = hv(fo[:, 0:HV])[:, :, 0:HD]
                    ch.seq(V.tensor_copy(feat, hv(bank[5][:, D:2 * D])))
                    ch.seq(V.tensor_tensor(hv(tmpel), feat, hv(v_al), ALU.mult))
                    ch.seq(V.tensor_reduce(fo[:, HV:FTW], hv(tmpel), AXX, ALU.add))
                    ch.seq(V.tensor_tensor(hv(tmpel), feat, hv(v_ar), ALU.mult))
                    ch.seq(V.tensor_reduce(ero, hv(tmpel), AXX, ALU.add))
                    ch.end()
                if on(3):
                    u = t - 3
                    ch = Chain(dve, S_["m_dve3"], 2)
                    ch.start(u)
                    dve.wait_ge(S_["m_mm2"], u + 1)
                    wait(dve, S_["m_sxh"], 16 * u)
                    ch.seq(V.tensor_tensor(hl, bank[4][:, D:2 * D], v_bl, ALU.add))
                    ch.seq(V.tensor_tensor(xh, xm, hl, ALU.add))
                    ch.end()
                if on(2):
                    u = t - 2
                    ch = Chain(dve, S_["m_dve2"], M2)
                    ch.start(u)
                    dve.wait_ge(S_["m_mm1"], u + 1)
                    ch.seq(V.tensor_tensor(z, bank[1][:, D:2 * D], v_b2, ALU.add))
                    ch.seq(V.tensor_tensor(z2, z, h1, ALU.add))
                    norm(ch, 2, z2, z, S_["m_var2"], S_["m_rs2"], u)
                    ch.seq(V.tensor_tensor(z2, z, v_g2, ALU.mult))
                    ch.seq(V.tensor_tensor(z, z2, v_b2n, ALU.add))
                    dve.wait_ge(S_["m_x"], 16 * (u + 1))
                    V.tensor_tensor(xm, xt, z, ALU.add).then_inc(S_["m_rdx"], 1)
                    dve.wait_ge(S_["m_rdx"], u + 1)
                    norm(ch, 3, xm, z2, S_["m_var3"], S_["m_rs3"], u)
                    ch.seq(V.tensor_scalar(h2, z2, 0.0, None, ALU.max))
                    ch.end()
                if on(1):
                    u = t - 1
                    ch = Chain(dve, S_["m_dve1"], M1)
                    ch.start(u)
                    dve.wait_ge(S_["m_mm0"], u + 1)
                    dve.wait_ge(S_["m_h"], 16 * (u + 1))
                    ch.seq(V.tensor_tensor(y, bank[0][:, D:2 * D], v_bp, ALU.add))
                    ch.seq(V.tensor_tensor(h1, y, ht, ALU.add))
                    norm(ch, 1, h1, y, S_["m_var1"], S_["m_rs1"], u)
                    ch.seq(V.tensor_tensor(h1, y, v_g1, ALU.mult))
                    ch.seq(V.tensor_tensor(h1, h1, v_b1n, ALU.add))
                    ch.end()
                if on(0):
                    ch = Chain(dve, S_["m_dve0"], M0)
                    ch.start(t)
                    dve.wait_ge(S_["m_acc"], 16 * (t + 1))
                    ch.seq(V.tensor_scalar(den[:, 0:H], hv(at_in)[:, :, HD], 1e-30, None, ALU.max))
                    ch.seq(V.reciprocal(den[:, H:2 * H], den[:, 0:H]))
                    V.tensor_tensor(hv(at), hv(at_in)[:, :, 0:HD],
                                    den[:, H:2 * H].unsqueeze(2).to_broadcast([P, H, HD]),
                                    ALU.mult).then_inc(S_["m_rdacc"], 1)
                    ch.end()

            for t in range(4):
                m_turn(t)
            with dve.Fori(4, NT) as t:
                m_turn(t)
            for t in range(NT, NT + 4):
                m_turn(t)

            edge_phase(1)

            dve.wait_ge(S_["m_w"], 16 * 16)
            cf = Chain(dve, S_["f_dve"], FIN)

            def f_turn(t, par, i):
                cf.start(t)
                dve.wait_ge(S_[f"f_acc{par}"], 16 * (i + 1))
                dve.wait_ge(S_[f"f_xh{par}"], 16 * (i + 1))
                wait(dve, S_[f"f_st{par}"], 16 * i)
                a, d, o = fin_a[par], fin_d[par], fin_o[par]
                cf.seq(V.tensor_scalar(d[:, 0:H], hv(fin_in[par])[:, :, HD], 1e-30, None, ALU.max))
                cf.seq(V.reciprocal(d[:, H:2 * H], d[:, 0:H]))
                cf.seq(V.tensor_tensor(hv(a), hv(fin_in[par])[:, :, 0:HD],
                                       d[:, H:2 * H].unsqueeze(2).to_broadcast([P, H, HD]), ALU.mult))
                cf.seq(V.tensor_tensor(o, a, v_gb, ALU.add))
                cf.seq(V.scalar_tensor_tensor(a, o, 0.01, o, ALU.mult, ALU.max))
                cf.seq(V.tensor_tensor(o, a, fin_xh[par], ALU.add))
                cf.end()

            with dve.Fori(0, NT // 2) as i:
                for par in range(2):
                    f_turn(2 * i + par, par, i)


_W = ["L0_gnn_Wq", "L0_gnn_Wk", "L0_gnn_Wv", "L0_gnn_Wp", "L0_gnn_bp", "L0_gnn_ln1_g", "L0_gnn_ln1_b",
      "L0_gnn_ln2_g", "L0_gnn_ln2_b", "L0_gnn_W1", "L0_gnn_b1", "L0_gnn_W2", "L0_gnn_b2",
      "L1_gnn_W_lin", "L1_gnn_b_lin", "L1_gnn_W_gat", "L1_gnn_attn_l", "L1_gnn_attn_r", "L1_gnn_gat_bias"]


def kernel(**inputs):
    import numpy as np
    import concourse.bacc as bacc
    from concourse.bass_utils import run_bass_kernel_spmd as run

    a = {k: np.ascontiguousarray(v) for k, v in inputs.items()}
    x = np.concatenate([a["x"], np.zeros((NPAD - N, D), np.float32)])
    pad = NSPAN * SPAN - E
    i32 = lambda n, v: np.full(n, v, np.int32)
    src = np.concatenate([a["src"], i32(pad + SPAN, 0)])
    dst = np.concatenate([a["dst"], i32(pad, NPAD - 1), i32(SPAN, NOWHERE)])
    prev = np.concatenate([i32(1, -1), dst[:-1]])
    bias = np.concatenate([a["edge_weight1"].reshape(-1).view(np.int32), i32(pad + SPAN, 0)])
    edges = np.stack([src, dst, prev, bias], -1).reshape(NSPAN + 1, 2, P, 4).transpose(0, 2, 1, 3)
    last = np.concatenate([dst[:NSPAN * SPAN].reshape(NSPAN, SPAN)[:, -1], i32(LC * P - NSPAN, 1 << 30)])
    arrays = {"x": x, "last": last, "edges": np.ascontiguousarray(edges.reshape(-1, 8))}
    arrays.update({n: a[n].reshape(-1) if a[n].shape == (H, HD) else a[n] for n in _W})
    nc = bacc.Bacc("TRN2", target_bir_lowering=False, num_devices=1)
    args = [nc.dram_tensor(f"in_{n}", v.shape, mybir.dt.from_np(v.dtype), kind="ExternalInput").ap()
            for n, v in arrays.items()]
    o = nc.dram_tensor("out_0", (N, D), F32, kind="ExternalOutput").ap()
    build(nc, *args, o)
    r = run(nc, [{f"in_{n}": v for n, v in arrays.items()}], core_ids=[0])
    return r.results[0]["out_0"]
```

```python
from contextlib import ExitStack

import concourse.bass as bass
from concourse import mybir

F32 = mybir.dt.float32
I32 = mybir.dt.int32
ALU = mybir.AluOpType
ACT = mybir.ActivationFunctionType
AXX = mybir.AxisListType.X

P = 128
N, D, H, E = 12500, 256, 8, 200000
HD = D // H
FFN = 4 * D
FC = FFN // P
NT = -(-N // P)
NPAD = NT * P
SPAN = 2 * P
NSPAN = -(-E // SPAN)
ST = 8
CH = 2 * ST
NB = -(-(NSPAN + NT) // ST)
NS = NB * ST
LC = -(-NSPAN // P)
HV = H * (HD + 1)
KVW = D + HV
FTW = HV + H
BIG = 1.0e30
EPS = 1e-5
NOWHERE = 1 << 20
RING = (2, 4)
assert NB % 2 == 0 and NB >= 6 and NS > NSPAN + NT - 1


class Chain:

    def __init__(self, eng, sem, per):
        self.eng, self.sem, self.per, self.k, self.n = eng, sem, per, 0, 0

    def start(self, n):
        self.k, self.n = 0, n

    def did(self, ins):
        ins.then_inc(self.sem, 1)
        self.k += 1

    def sync(self):
        self.eng.wait_ge(self.sem, self.n * self.per + self.k)

    def seq(self, ins):
        self.did(ins)
        self.sync()

    def end(self):
        assert self.k == self.per, (self.k, self.per)


class Blk:

    def __init__(self, n, quad, lap4, ring):
        self.n, self.quad, self.lap4, self.ring = n, quad, lap4, ring
        self.par, self.half = quad % 2, lap4 * 2 + quad // 2
        self.slot, self.lap = (self.par, self.half) if ring == 2 else (quad, lap4)

    def next(self):
        return Blk(self.n + 1, (self.quad + 1) % 4, self.lap4 + (self.quad + 1) // 4, self.ring)

    def prev(self):
        return Blk(self.n - 1, (self.quad - 1) % 4, self.lap4 - (1 if self.quad == 0 else 0), self.ring)


def blk_at(b, layer):
    return Blk(b, b % 4, b // 4, RING[layer])


def blocks(eng, layer, turn):
    whole = (NB - 2) // 4
    for b in range(4):
        turn(blk_at(b, layer))
    with eng.Fori(1, whole) as i:
        for k in range(4):
            turn(Blk(i * 4 + k, k, i, RING[layer]))
    for b in range(whole * 4, NB):
        turn(blk_at(b, layer))


def tiles(eng, turn):
    for t in range(4):
        turn(t, t % 2, t // 2)
    with eng.Fori(2, NT // 2) as i:
        for par in range(2):
            turn(2 * i + par, par, i)
    turn(NT, 0, NT // 2)
    turn(NT + 1, 1, NT // 2)


def wait(eng, sem, count):
    if isinstance(count, int) and count <= 0:
        return
    eng.wait_ge(sem, count)


def build(nc, x, last, edges, Wq, Wk, Wv, Wp, bp, g1, b1n, g2, b2n, W1, b1, W2, b2,
          Wl, bl, Wg, al, ar, gb, out):
    ctx = ExitStack()
    with ctx:
        def sb(name, shape, dt=F32):
            return ctx.enter_context(nc.sbuf_tensor(name, shape, dt))

        def sem(name):
            return ctx.enter_context(nc.semaphore(name))

        def dram(name, shape):
            return nc.dram_tensor(name, shape, F32, kind="Internal").ap()

        kv_tab = dram("kv_tab", (NPAD, KVW))
        q_tab = dram("q_tab", (NPAD, D))
        h_tab = dram("h_tab", (NPAD, D))
        ft_tab = dram("ft_tab", (NPAD, FTW))
        er_tab = dram("er_tab", (NPAD, H))
        xh_tab = dram("xh_tab", (NPAD, D))
        sums = dram("sums", (NS * P, HV))

        ident = sb("ident", [P, P])
        ones = sb("ones", [P, P])
        lane = sb("lane", [P, P])
        steps = sb("steps", [P, NS])
        spanid = sb("spanid", [P, LC])
        tile_of = sb("tile_of", [P, NS])
        same = sb("same", [P, NS])
        tile_row = sb("tile_row", [1, NS], I32)
        endstep = sb("endstep", [1, NT], I32)
        endf = sb("endf", [1, NT])
        last_i = sb("last_i", [P, LC], I32)
        last_t = sb("last_t", [P, LC], I32)
        last_f = sb("last_f", [P, LC])
        last_s = sb("last_s", [P, LC])
        mhalf = sb("mhalf", [P, 1])

        GW = max(RING[0] * CH * KVW, RING[1] * CH * FTW)
        Gf = sb("Gf", [P, GW])[:, :]
        rows = [[Gf[:, k * CH * w:(k + 1) * CH * w].rearrange("p (c w) -> p c w", c=CH) for k in range(n)]
                for n, w in ((RING[0], KVW), (RING[1], FTW))]
        ef = sb("ef", [P, 2, CH, 4], I32)
        qs = sb("qs", [P, 2, ST, D])
        oh = sb("oh", [P, 4, CH, P])
        oht = sb("oht", [P, 2, 4, P])
        oh0 = sb("oh0", [P, 2])
        prod = sb("prod", [P, 3, 2, D])
        absd = sb("absd", [P, 2, 4, P])
        ev = sb("ev", [P, 4, 2, HV])
        acc = sb("acc", [P, 2, ST, HV])
        accr = sb("accr", [P, HV])
        dloc = sb("dloc", [P, 2, CH])
        samec = sb("samec", [P, 2, ST])
        lk = sb("lk", [P, 2, CH])
        msk = sb("msk", [P, 3, CH])
        bm = sb("bm", [P, CH])
        arep = sb("arep", [P, P])
        ats = sb("ats", [P, P + 1])
        sred = sb("sred", [P, P])
        S = sb("S", [P, P])
        scan1 = sb("scan1", [P, P])
        scan2 = sb("scan2", [P, P])
        v4 = sb("v4", [P, 2])
        rowS = sb("rowS", [1, 4, P])
        d0f = sb("d0f", [1, P])
        d1f = sb("d1f", [1, P])
        d0b = sb("d0b", [1, P])
        d1b = sb("d1b", [1, P])
        inr = sb("inr", [1, P])
        outr = sb("outr", [1, P])
        carry = sb("carry", [1, H])
        ct = sb("ct", [1, 5, H])
        rexp = sb("rexp", [1, H])
        cols = sb("cols", [P, 2])
        rt = sb("rt", [P, H])
        rm = sb("rm", [P, 2, H])
        df = sb("df", [P, P])
        ex = sb("ex", [P, 2, P])

        bank = [ctx.enter_context(nc.psum_tensor(f"bank{i}", [P, 512], F32)) for i in range(8)]

        used = [0]

        def carve(n):
            a = used[0]
            used[0] += n
            assert used[0] <= GW
            return Gf[:, a:a + n]

        st = sb("st", [P, 4, 6])
        mv = sb("mv", [P, 4, 2])
        vr = sb("vr", [P, 8])

        w_v = carve(2 * D).rearrange("p (k n) -> p k n", k=2)
        w_kq = carve(4 * D).rearrange("p (k n) -> p k n", k=2)
        xts, hts, hTs, kvos, qos, qns = [[carve(w) for _ in range(2)] for w in (D, D, D, KVW, D, D)]

        used[0] = 0
        w_p = carve(2 * D).rearrange("p (k n) -> p k n", k=2)
        w_1 = carve(2 * FFN).rearrange("p (k n) -> p k n", k=2)
        w_2 = carve(FC * D).rearrange("p (k n) -> p k n", k=FC)
        w_l = carve(2 * D).rearrange("p (k n) -> p k n", k=2)
        w_g = carve(2 * D).rearrange("p (k n) -> p k n", k=2)
        v_bp, v_g1, v_b1n, v_g2, v_b2n, v_b2, v_bl, v_al, v_ar = [carve(D) for _ in range(9)]
        v_b1 = carve(FC)
        xt, ht = carve(D), carve(D)
        at_in, at, atT, den = carve(HV), carve(D), carve(D), carve(2 * H)
        y, h1, h1T, gT = carve(D), carve(D), carve(D), carve(FFN)
        z, z2, xm, h2, h2T, hl, hlT, xh = [carve(D) for _ in range(8)]
        fo, tmpel, ero = carve(FTW), carve(D), carve(H)

        used[0] = 0
        v_gb = carve(D)
        fin_in, fin_xh, fin_a, fin_o, fin_d = [[carve(w) for _ in range(2)] for w in (HV, D, D, D, 2 * H)]

        ohf = oh[:, :, :, :].rearrange("p a c n -> p (a c n)")
        qsf = qs[:, :, :, :].rearrange("p a s n -> p (a s n)")
        cmp_ = [(ohf if c < 4 else qsf)[:, (c % 4) * NS:(c % 4 + 1) * NS] for c in range(LC)]
        cmpe = [ev[:, :, :, :].rearrange("p a k n -> p (a k n)")[:, c * NT:(c + 1) * NT] for c in range(LC)]
        S_ = {}
        for name in """const_made gather_free stats_made setup_loaded path_dve path_pe w_loaded
            q_x0 q_x1 q_dve q_rstd q_relu q_tr q_hT q_mm q_ka q_st0 q_st1 q_sh0 q_sh1 q_vq
            m_w m_acc m_h m_x m_dve0 m_dve1 m_dve2 m_dve3 m_dve4 m_var1 m_var2 m_var3 m_rs1 m_rs2 m_rs3
            m_tr0 m_tr1 m_tr2 m_tr3 m_cp0 m_cp1 m_cp2 m_cp3 m_mm0 m_mm1 m_mm2 m_mm3 m_w1 m_gelu
            m_sxh m_sft m_rdacc m_rdx f_acc0 f_acc1 f_xh0 f_xh1 f_dve f_st0 f_st1""".split():
            S_[name] = sem(name)
        L_ = []
        for layer in range(2):
            d = {}
            for name in """fld samec_made ohd arep_made oh_made pat ats_made oht_tr oht_cp qexp prodd redd smade
                s_tr soft v4_made oh0_made rows_mm rows_cp row rowsdone cols_mm cols_cp r_exp bm_made
                m_made m_tr dmade ex_made ev_made agg accd resc init""".split():
                d[name] = sem(f"{name}_{layer}")
            d["efl"] = [sem(f"efl{layer}{p}") for p in range(2)]
            d["acs"] = [sem(f"acs{layer}{p}") for p in range(2)]
            d["gat"] = ([[sem(f"gat{p}_{s}") for s in range(ST)] for p in range(2)] if layer == 0
                        else [[sem(f"gath{k}")] for k in range(RING[1])])
            L_.append(d)

        FLD, SOFT, ROW = 6, 6, 13
        M0, M1, M2 = 2, 7, 11
        QN = 3
        FIN = 6
        block = ctx.enter_context(nc.Block())

        def hc(ap):
            return ap.rearrange("p (h c) -> p h c", h=H)

        def hv(ap):
            return ap.rearrange("p (h w) -> p h w", h=H)

        @block.sync
        def _(sp):
            sp.dma_start(last_i[:, :], last.rearrange("(p c) -> p c", c=LC)).then_inc(S_["setup_loaded"], 16)
            for w, src in ((w_v, Wv), (w_kq[:, :, 0:D], Wk), (w_kq[:, :, D:2 * D], Wq)):
                sp.dma_start(w, src.rearrange("(k p) n -> p k n", p=P)).then_inc(S_["w_loaded"], 16)

            def q_load(t, par):
                wait(sp, S_["q_dve"], QN * (t - 1))
                sp.dma_start(xts[par], x[bass.ds(t * P, P), :]).then_inc(S_[f"q_x{par}"], 16)

            def q_store(t, par):
                sp.wait_ge(S_["q_relu"], t + 1)
                sp.dma_start(h_tab[bass.ds(t * P, P), :], hts[par]).then_inc(S_[f"q_sh{par}"], 16)
                sp.wait_ge(S_["q_vq"], t + 1)
                sp.wait_ge(S_["q_ka"], 2 * t + 2)
                sp.dma_start(kv_tab[bass.ds(t * P, P), :], kvos[par]).then_inc(S_[f"q_st{par}"], 16)
                sp.dma_start(q_tab[bass.ds(t * P, P), :], qos[par]).then_inc(S_[f"q_st{par}"], 16)

            for t in range(3):
                q_load(t, t % 2)
            q_load(3, 1)
            q_store(0, 0)
            with sp.Fori(0, NT // 2 - 2) as i:
                for par in range(2):
                    q_load(2 * i + par + 4, par)
                    q_store(2 * i + par + 1, 1 - par)
            for t in range(NT - 3, NT):
                q_store(t, t % 2)
            for par in range(2):
                sp.wait_ge(S_[f"q_sh{par}"], 16 * (NT // 2))
                sp.wait_ge(S_[f"q_st{par}"], 32 * (NT // 2))
            sp.wait_ge(S_["path_dve"], 1)

            def edge_loads(L, layer, B):
                wait(sp, L["smade"], B.n - 1)
                for s in range(ST):
                    step = B.n * ST + s
                    t = sp.value_load(tile_row[0:1, bass.ds(step, 1)], min_val=0, max_val=NT - 1)
                    m = nc.s_assert_within(sp.snap(step - t), 0, NSPAN,
                                           skip_runtime_bounds_check_because="step = span + tile")
                    sp.dma_start(ef[:, B.par, 2 * s:2 * s + 2, :],
                                 edges[bass.ds(m * P, P), :].rearrange("p (k f) -> p k f", f=4)
                                 ).then_inc(L["efl"][B.par], 16)
                    tab, w = (q_tab, D) if layer == 0 else (er_tab, H)
                    sp.dma_start(qs[:, B.par, s, 0:w], tab[bass.ds(t * P, P), :]).then_inc(L["efl"][B.par], 16)

            def edge_phase(layer):
                L = L_[layer]
                blocks(sp, layer, lambda B: edge_loads(L, layer, B))
                for par in range(2):
                    sp.wait_ge(L["acs"][par], 16 * ST * (NB // 2))

            edge_phase(0)

            for w, src in ((w_p, Wp), (w_1, W1), (w_2, W2), (w_l, Wl), (w_g, Wg)):
                sp.dma_start(w, src.rearrange("(k p) n -> p k n", p=P)).then_inc(S_["m_w"], 16)
            for v, src in ((v_bp, bp), (v_g1, g1), (v_b1n, b1n), (v_g2, g2), (v_b2n, b2n), (v_b2, b2),
                           (v_bl, bl), (v_al, al), (v_ar, ar)):
                sp.dma_start(v, src.partition_broadcast(P)).then_inc(S_["m_w"], 16)
            sp.dma_start(v_b1, b1.rearrange("(c p) -> p c", p=P), allow_slow_non_contiguous=True).then_inc(S_["m_w"], 16)

            def m_turn(t):
                if not isinstance(t, int) or t < NT:
                    wait(sp, S_["m_rdacc"], t)
                    e = sp.value_load(endstep[0:1, bass.ds(t, 1)], min_val=0, max_val=NS - 1)
                    sp.dma_start(at_in, sums[bass.ds(e * P, P), :]).then_inc(S_["m_acc"], 16)
                if not isinstance(t, int) or 1 <= t <= NT:
                    wait(sp, S_["m_var1"], t - 1)
                    sp.dma_start(ht, h_tab[bass.ds((t - 1) * P, P), :]).then_inc(S_["m_h"], 16)
                if not isinstance(t, int) or 2 <= t <= NT + 1:
                    wait(sp, S_["m_rdx"], t - 2)
                    sp.dma_start(xt, x[bass.ds((t - 2) * P, P), :]).then_inc(S_["m_x"], 16)
                if not isinstance(t, int) or 3 <= t <= NT + 2:
                    u = t - 3
                    sp.wait_ge(S_["m_dve3"], 2 * u + 2)
                    sp.dma_start(xh_tab[bass.ds(u * P, P), :], xh).then_inc(S_["m_sxh"], 16)
                if not isinstance(t, int) or t >= 4:
                    u = t - 4
                    sp.wait_ge(S_["m_dve4"], 5 * u + 5)
                    sp.dma_start(ft_tab[bass.ds(u * P, P), :], fo).then_inc(S_["m_sft"], 16)
                    sp.dma_start(er_tab[bass.ds(u * P, P), :], ero).then_inc(S_["m_sft"], 16)

            for t in range(5):
                m_turn(t)
            with sp.Fori(5, NT) as t:
                m_turn(t)
            for t in range(NT, NT + 4):
                m_turn(t)
            sp.wait_ge(S_["m_sxh"], 16 * NT)
            sp.wait_ge(S_["m_sft"], 32 * NT)

            edge_phase(1)

            sp.dma_start(v_gb, gb.partition_broadcast(P)).then_inc(S_["m_w"], 16)

            def f_load(t, par, i):
                wait(sp, S_["f_dve"], FIN * (t - 1))
                e = sp.value_load(endstep[0:1, bass.ds(t, 1)], min_val=0, max_val=NS - 1)
                sp.dma_start(fin_in[par], sums[bass.ds(e * P, P), :]).then_inc(S_[f"f_acc{par}"], 16)
                sp.dma_start(fin_xh[par], xh_tab[bass.ds(t * P, P), :]).then_inc(S_[f"f_xh{par}"], 16)

            def f_store(t, par, rows):
                sp.wait_ge(S_["f_dve"], FIN * (t + 1))
                sp.dma_start(out[bass.ds(t * P, rows), :], fin_o[par][0:rows, :]).then_inc(S_[f"f_st{par}"], 16)

            f_load(0, 0, 0)
            f_load(1, 1, 0)
            with sp.Fori(0, NT // 2 - 1) as i:
                for par in range(2):
                    f_load(2 * i + par + 2, par, i)
                    f_store(2 * i + par, par, P)
            f_store(NT - 2, 0, P)
            f_store(NT - 1, 1, N - (NT - 1) * P)
            for par in range(2):
                sp.wait_ge(S_[f"f_st{par}"], 16 * (NT // 2))

        @block.gpsimd
        def _(pool):
            cm = S_["const_made"]
            pool.memset(ident[:, :], 0.0).then_inc(cm, 1)
            pool.memset(ones[:, :], 1.0).then_inc(cm, 1)
            pool.memset(mhalf[:, :], -0.5).then_inc(cm, 1)
            pool.wait_ge(cm, 3)
            pool.affine_select(out=ident[:, :], in_=ident[:, :], compare_op=ALU.not_equal, fill=1.0,
                               base=0, pattern=[[-1, P]], channel_multiplier=1).then_inc(cm, 1)
            pool.iota(lane[:, :], [[1, P]], base=0, channel_multiplier=0,
                      allow_small_or_imprecise_dtypes=True).then_inc(cm, 1)
            pool.iota(steps[:, :], [[1, NS]], base=0, channel_multiplier=0,
                      allow_small_or_imprecise_dtypes=True).then_inc(cm, 1)
            pool.iota(spanid[:, :], [[1, LC]], base=0, channel_multiplier=LC,
                      allow_small_or_imprecise_dtypes=True).then_inc(cm, 1)

            def rstd(k, ready, n, done):
                pool.wait_ge(ready, n + 1)
                pool.tensor_tensor(vr[:, 2 * k + 1:2 * k + 2], vr[:, 2 * k:2 * k + 1], mhalf[:, :],
                                   ALU.pow).then_inc(done, 1)

            pool.wait_ge(cm, 7)
            with pool.Fori(0, NT) as t:
                rstd(0, S_["q_rstd"], 2 * t, S_["q_rstd"])

            def edge_phase(layer):
                L = L_[layer]
                tab = (kv_tab, ft_tab)[layer]

                def turn(B):
                    pool.wait_ge(L["efl"][B.par], 32 * ST * (B.half + 1))
                    for c in range(CH):
                        free = (B.n - B.ring) * ST + c // 2 + 1
                        if c % 2 == 0 and not (isinstance(free, int) and free <= 0):
                            pool.wait_ge(L["ev_made"], free)
                            pool.sem_inc(S_["gather_free"], 1)
                        elif c == 0:
                            pool.sem_inc(S_["gather_free"], 1)
                        pool.indirect_dma_start(
                            out=rows[layer][B.slot][:, c, :], out_offset=None, in_=tab,
                            in_offset=bass.IndirectOffsetOnAxis(ap=ef[:, B.par, c, 0:1], axis=0),
                        ).then_inc(L["gat"][B.slot][c // 2 if layer == 0 else 0], 16)

                blocks(pool, layer, turn)

            edge_phase(0)

            for t in range(5):
                for k in (2, 3, 1):
                    first = 1 if k == 1 else 2
                    if first <= t:
                        rstd(k, S_[f"m_var{k}"], t - first, S_[f"m_rs{k}"])
            with pool.Fori(5, NT) as t:
                for k in (2, 3, 1):
                    rstd(k, S_[f"m_var{k}"], t - (1 if k == 1 else 2), S_[f"m_rs{k}"])
            for t in range(NT, NT + 2):
                for k in (2, 3, 1):
                    first = 1 if k == 1 else 2
                    if t < NT + first:
                        rstd(k, S_[f"m_var{k}"], t - first, S_[f"m_rs{k}"])
            edge_phase(1)

        @block.scalar
        def _(act):
            def copy(o, i_, s):
                act.activation(o, i_, ACT.Copy).then_inc(s, 1)

            act.wait_ge(S_["const_made"], 7)

            def q_turn(t, par, i):
                q = 1 - par
                if not isinstance(t, int) or t < NT:
                    act.wait_ge(S_["q_dve"], QN * (t + 1))
                    wait(act, S_[f"q_sh{par}"], 16 * i)
                    act.activation(hts[par], qns[par], ACT.Relu).then_inc(S_["q_relu"], 1)
                if not isinstance(t, int) or 1 <= t <= NT:
                    act.wait_ge(S_["q_tr"], t)
                    wait(act, S_["q_mm"], t - 2)
                    copy(hTs[q], bank[q][:, 0:D], S_["q_hT"])
                if not isinstance(t, int) or t >= 2:
                    act.wait_ge(S_["q_mm"], t - 1)
                    wait(act, S_[f"q_st{par}"], 32 * (i - 1))
                    copy(kvos[par][:, 0:D], bank[2 + par][:, 0:D], S_["q_ka"])
                    copy(qos[par], bank[2 + par][:, D:2 * D], S_["q_ka"])

            tiles(act, q_turn)

            def onehots(L, B, g):
                n = B.n * 4 + g
                act.wait_ge(L["fld"], FLD * (B.n + 1))
                wait(act, L["agg"], (B.n - 4) * ST + 2 * g + 2)
                wait(act, L["oh_made"], n - 1)
                for k in range(4):
                    act.activation(absd[:, g % 2, k, :], lane[:, :], ACT.Abs, scale=-1.0,
                                   bias=dloc[:, B.par, 4 * g + k:4 * g + k + 1]).then_inc(L["ohd"], 1)
                act.wait_ge(L["ohd"], 4 * n + 4)
                act.activation(oh[:, B.quad, 4 * g:4 * g + 4, :].rearrange("p c n -> p (c n)"),
                               absd[:, g % 2, :, :].rearrange("p c n -> p (c n)"), ACT.Relu, scale=-1.0,
                               bias=ones[:, 0:1]).then_inc(L["oh_made"], 1)

            def turned(L, B, g):
                act.wait_ge(L["oht_tr"], B.n * 4 + g + 1)
                wait(act, L["qexp"], B.n * ST + 2 * g - 2)
                if g == 2:
                    act.wait_ge(L["oh0_made"], B.n + 1)
                copy(oht[:, g % 2, :, :].rearrange("p c n -> p (c n)"), bank[g % 2][:, :], L["oht_cp"])
                if g == 0:
                    act.wait_ge(L["oht_cp"], B.n * 4 + 1)
                    wait(act, L["soft"], SOFT * (B.n - 1))
                    copy(oh0[:, B.par:B.par + 1], oht[:, 0, 0, 0:1], L["oh0_made"])

            def edge_phase(layer):
                L = L_[layer]

                def sum_store(B, s):
                    act.wait_ge(L["accd"], B.n * ST + s + 1)
                    act.dma_start(sums[bass.ds((B.n * ST + s) * P, P), :],
                                  acc[:, B.par, s, :]).then_inc(L["acs"][B.par], 16)

                def turn(B):
                    b = B.n
                    more = not (isinstance(b, int) and b == NB - 1)

                    def stored(*ss):
                        if not (isinstance(b, int) and b == 0):
                            for s in ss:
                                sum_store(B.prev(), s)

                    act.wait_ge(L["pat"], b + 1)
                    wait(act, L["soft"], SOFT * b)
                    copy(ats[:, 0:P], bank[7][:, 0:P], L["ats_made"])
                    if layer == 0:
                        turned(L, B, 2)
                        turned(L, B, 3)
                    if more:
                        onehots(L, B.next(), 0)
                        onehots(L, B.next(), 1)
                    act.wait_ge(L["rows_mm"], b + 1)
                    copy(rowS[:, :, :].rearrange("p q n -> p (q n)"), bank[7][0:1, :], L["rows_cp"])
                    if more:
                        onehots(L, B.next(), 2)
                    act.wait_ge(L["row"], ROW * b + ROW)
                    act.activation(rexp[:, :], ct[:, 4, :], ACT.Exp).then_inc(L["r_exp"], 1)
                    act.wait_ge(L["cols_mm"], b + 1)
                    copy(cols[:, :], bank[7][:, 0:2], L["cols_cp"])
                    if more:
                        onehots(L, B.next(), 3)
                    act.wait_ge(L["dmade"], b + 1)
                    act.activation(ex[:, B.par, :], df[:, :], ACT.Exp).then_inc(L["ex_made"], 1)
                    if more:
                        turned(L, B.next(), 0)
                    stored(0, 1, 2, 3)
                    if more:
                        turned(L, B.next(), 1)
                    stored(4, 5)
                    if more and layer == 1:
                        turned(L, B.next(), 2)
                        turned(L, B.next(), 3)
                    stored(6, 7)

                z = blk_at(0, layer)
                for g in range(4):
                    onehots(L, z, g)
                for g in range(4 if layer == 1 else 2):
                    turned(L, z, g)
                blocks(act, layer, turn)
                for s in range(ST):
                    sum_store(blk_at(NB - 1, layer), s)

            edge_phase(0)

            act.wait_ge(S_["m_w"], 16 * 15)

            def m_turn(t):
                def on(k):
                    return not isinstance(t, int) or k <= t < NT + k
                for k, dst, b in ((3, hlT, 5), (2, h2T, 4)):
                    if on(k):
                        act.wait_ge(S_[f"m_tr{k}"], t - k + 1)
                        copy(dst, bank[b][:, 0:D], S_[f"m_cp{k}"])
                if on(1):
                    u = t - 1
                    act.wait_ge(S_["m_tr1"], u + 1)
                    copy(h1T, bank[1][:, 0:D], S_["m_cp1"])
                    for f in range(FC):
                        if f % 4 == 0:
                            act.wait_ge(S_["m_w1"], 2 * u + f // 4 + 1)
                        act.activation(gT[:, f * P:(f + 1) * P], bank[2 + f // 4][:, (f % 4) * P:(f % 4 + 1) * P],
                                       ACT.Gelu, bias=v_b1[:, f:f + 1]).then_inc(S_["m_gelu"], 1)
                if on(0):
                    act.wait_ge(S_["m_tr0"], t + 1)
                    copy(atT, bank[0][:, 0:D], S_["m_cp0"])

            for t in range(5):
                m_turn(t)
            with act.Fori(5, NT) as t:
                m_turn(t)
            for t in range(NT, NT + 4):
                m_turn(t)

            edge_phase(1)

        @block.tensor
        def _(pe):
            def mm(o, a, r, first=True, end=True):
                return nc.tensor.matmul(o, a, r, start=first, stop=end)

            def tr(o, i_):
                return nc.tensor.transpose(o, i_, ident[:, :])

            pe.wait_ge(S_["const_made"], 7)
            pe.wait_ge(S_["path_pe"], 2 * LC)
            half = NS // 2
            for c in range(LC):
                for k in range(2):
                    mm(bank[4 + k][:, 0:half], ones[:, :], cmp_[c][:, k * half:(k + 1) * half],
                       c == 0, c == LC - 1)
                m = mm(bank[6][:, 0:NT], ones[:, :], cmpe[c], c == 0, c == LC - 1)
            m.then_inc(S_["path_pe"], 1)

            pe.wait_ge(S_["w_loaded"], 48)

            def q_turn(t, par, i):
                if not isinstance(t, int) or 1 <= t <= NT:
                    q = 1 - par
                    pe.wait_ge(S_["q_relu"], t)
                    wait(pe, S_["q_hT"], t - 2)
                    tr(bank[q][:, 0:P], hts[q][:, 0:P])
                    tr(bank[q][:, P:D], hts[q][:, P:D]).then_inc(S_["q_tr"], 1)
                if not isinstance(t, int) or t >= 2:
                    pe.wait_ge(S_["q_hT"], t - 1)
                    wait(pe, S_["q_vq"], t - 3)
                    wait(pe, S_["q_ka"], 2 * (t - 3))
                    for k in range(2):
                        mm(bank[2 + par][:, :], hTs[par][:, k * P:(k + 1) * P], w_kq[:, k, :], k == 0, k == 1)
                    for k in range(2):
                        m = mm(bank[4 + par][:, 0:D], hTs[par][:, k * P:(k + 1) * P], w_v[:, k, :], k == 0, k == 1)
                    m.then_inc(S_["q_mm"], 1)

            tiles(pe, q_turn)

            def turns(L, B, g):
                pe.wait_ge(L["oh_made"], B.n * 4 + g + 1)
                wait(pe, L["oht_cp"], B.n * 4 + g - 1)
                for k in range(4):
                    m = tr(bank[g % 2][:, k * P:(k + 1) * P], oh[:, B.quad, 4 * g + k, :])
                m.then_inc(L["oht_tr"], 1)

            def spread(L, layer, B, s):
                if s == 0:
                    pe.wait_ge(L["efl"][B.par], 32 * ST * (B.half + 1))
                if s % 2 == 0:
                    pe.wait_ge(L["oht_cp"], B.n * 4 + s // 2 + 1)
                if layer == 0:
                    wait(pe, L["prodd"], B.n * ST + s - 1)
                elif s == 0:
                    wait(pe, L["smade"], B.n - 1)
                for k in range(2):
                    a = oht[:, (s // 2) % 2, 2 * (s % 2) + k, :]
                    if layer == 0:
                        m = mm(bank[2 + s % 2][:, k * D:(k + 1) * D], a, qs[:, B.par, s, :])
                    else:
                        c = 2 * s + k
                        m = mm(bank[2 + B.par][:, c * H:(c + 1) * H], a, qs[:, B.par, s, 0:H])
                m.then_inc(L["qexp"], 1)

            def agg(L, B, s):
                pe.wait_ge(L["ev_made"], B.n * ST + s + 1)
                wait(pe, L["accd"], B.n * ST + s - 1)
                o = bank[4 + s % 2][:, 0:HV]
                mm(o, oh[:, B.quad, 2 * s, :], ev[:, s % 4, 0, :], True, False)
                mm(o, oh[:, B.quad, 2 * s + 1, :], ev[:, s % 4, 1, :], False, True).then_inc(L["agg"], 1)

            def edge_phase(layer):
                L = L_[layer]

                def turn(B):
                    b = B.n
                    first = isinstance(b, int) and b == 0
                    last_ = isinstance(b, int) and b == NB - 1

                    def aggs(*ss):
                        if not first:
                            for s in ss:
                                agg(L, B.prev(), s)

                    pe.wait_ge(L["arep_made"], b + 1)
                    wait(pe, L["ats_made"], b)
                    wait(pe, L["soft"], SOFT * b)
                    tr(bank[7][:, 0:P], arep[:, :]).then_inc(L["pat"], 1)
                    if layer == 0:
                        turns(L, B, 2)
                        spread(L, layer, B, 2)
                        spread(L, layer, B, 3)
                        turns(L, B, 3)
                        for s in range(4, ST):
                            spread(L, layer, B, s)
                    pe.wait_ge(L["smade"], b + 1)
                    tr(bank[6][:, 0:P], S[:, :]).then_inc(L["s_tr"], 1)
                    aggs(0, 1)
                    pe.wait_ge(L["v4_made"], 2 * b + 2)
                    pe.wait_ge(L["soft"], SOFT * b + 2)
                    for q, v in enumerate((scan1[:, P - 1:P], scan2[:, 0:1], v4[:, 0:1], v4[:, 1:2])):
                        m = mm(bank[7][0:1, q * P:(q + 1) * P], v, ident[:, :])
                    m.then_inc(L["rows_mm"], 1)
                    aggs(2, 3)
                    pe.wait_ge(L["row"], ROW * b + ROW)
                    pe.wait_ge(L["r_exp"], b + 1)
                    mm(bank[7][:, 0:1], inr[0:1, :], ones[0:1, 0:1])
                    mm(bank[7][:, 1:2], outr[0:1, :], ones[0:1, 0:1])
                    mm(bank[7][:, 8:8 + H], ones[0:1, :], rexp[0:1, :]).then_inc(L["cols_mm"], 1)
                    nx = None if last_ else B.next()
                    if nx:
                        turns(L, nx, 0)
                    aggs(4, 5)
                    pe.wait_ge(L["soft"], SOFT * b + 4)
                    tr(bank[6][:, P:2 * P], scan2[:, :]).then_inc(L["m_tr"], 1)
                    if nx:
                        turns(L, nx, 1)
                    aggs(6)
                    if nx:
                        spread(L, layer, nx, 0)
                        spread(L, layer, nx, 1)
                    aggs(7)
                    if nx and layer == 1:
                        turns(L, nx, 2)
                        spread(L, layer, nx, 2)
                        spread(L, layer, nx, 3)
                        turns(L, nx, 3)
                        for s in range(4, ST):
                            spread(L, layer, nx, s)

                z = blk_at(0, layer)
                turns(L, z, 0)
                turns(L, z, 1)
                spread(L, layer, z, 0)
                spread(L, layer, z, 1)
                if layer == 1:
                    turns(L, z, 2)
                    spread(L, layer, z, 2)
                    spread(L, layer, z, 3)
                    turns(L, z, 3)
                    for s in range(4, ST):
                        spread(L, layer, z, s)
                blocks(pe, layer, turn)
                for s in range(ST):
                    agg(L, blk_at(NB - 1, layer), s)

            edge_phase(0)
            pe.wait_ge(S_["m_w"], 16 * 15)

            def m_turn(t):
                def on(k):
                    return not isinstance(t, int) or k <= t < NT + k

                def stage(k, src, dst, b, w, ready, count):
                    pe.wait_ge(ready, count)
                    tr(bank[b][:, 0:P], src[:, 0:P])
                    tr(bank[b][:, P:D], src[:, P:D]).then_inc(S_[f"m_tr{k}"], 1)
                    pe.wait_ge(S_[f"m_cp{k}"], t - k + 1)
                    if w is not None:
                        for c in range(2):
                            m = mm(bank[b][:, D:2 * D], dst[:, c * P:(c + 1) * P], w[:, c, :], c == 0, c == 1)
                        m.then_inc(S_[f"m_mm{k}"], 1)

                if on(3):
                    stage(3, hl, hlT, 5, w_g, S_["m_dve3"], 2 * (t - 3) + 2)
                if on(2):
                    stage(2, h2, h2T, 4, w_l, S_["m_dve2"], M2 * (t - 2) + M2)
                if on(1):
                    u = t - 1
                    stage(1, h1, h1T, 1, None, S_["m_dve1"], M1 * u + M1)
                    for f in range(FC):
                        for c in range(2):
                            m = mm(bank[2 + f // 4][:, (f % 4) * P:(f % 4 + 1) * P],
                                   w_1[:, c, f * P:(f + 1) * P], h1T[:, c * P:(c + 1) * P], c == 0, c == 1)
                        if f % 4 == 3:
                            m.then_inc(S_["m_w1"], 1)
                    for f in range(FC):
                        pe.wait_ge(S_["m_gelu"], FC * u + f + 1)
                        m = mm(bank[1][:, D:2 * D], gT[:, f * P:(f + 1) * P], w_2[:, f, :], f == 0, f == FC - 1)
                    m.then_inc(S_["m_mm1"], 1)
                if on(0):
                    stage(0, at, atT, 0, w_p, S_["m_rdacc"], t + 1)

            for t in range(5):
                m_turn(t)
            with pe.Fori(5, NT) as t:
                m_turn(t)
            for t in range(NT, NT + 4):
                m_turn(t)
            edge_phase(1)

        @block.vector
        def _(dve):
            V = nc.vector
            dve.wait_ge(S_["const_made"], 7)
            dve.wait_ge(S_["setup_loaded"], 16)
            c0 = Chain(dve, L_[0]["init"], 99)
            c0.start(0)
            c0.did(V.memset(ats[:, P:P + 1], 0.0))
            c0.did(V.memset(d0f[:, :], -BIG))
            c0.did(V.memset(d0b[:, :], -BIG))
            c0.did(V.memset(d1b[:, :], -BIG))
            c0.did(V.memset(carry[:, :], -BIG))
            c0.did(V.memset(acc[:, 1, ST - 1, :], 0.0))
            for kvo in kvos:
                c0.did(V.memset(kvo[:, D:KVW], 1.0))
            c0.seq(V.tensor_scalar(last_t[:, :], last_i[:, :], 7, None, ALU.logical_shift_right))
            c0.seq(V.tensor_copy(last_f[:, :], last_t[:, :]))
            c0.seq(V.tensor_tensor(last_s[:, :], last_f[:, :], spanid[:, :], ALU.add))
            for c in range(LC):
                V.tensor_scalar(cmp_[c], steps[:, :], last_s[:, c:c + 1], None,
                                ALU.is_gt).then_inc(S_["path_pe"], 1)
                V.tensor_scalar(cmpe[c], steps[:, 0:NT], last_f[:, c:c + 1], None,
                                ALU.is_ge).then_inc(S_["path_pe"], 1)
            dve.wait_ge(S_["path_pe"], 2 * LC + 1)
            half = NS // 2
            for k in range(2):
                c0.seq(V.tensor_tensor(tile_of[:, k * half:(k + 1) * half], steps[:, k * half:(k + 1) * half],
                                       bank[4 + k][:, 0:half], ALU.subtract))
            c0.seq(V.memset(same[:, 0:1], 0.0))
            c0.seq(V.tensor_tensor(same[:, 1:NS], tile_of[:, 1:NS], tile_of[:, 0:NS - 1], ALU.is_equal))
            c0.seq(V.tensor_tensor(endf[:, :], bank[6][0:1, 0:NT], steps[0:1, 0:NT], ALU.add))
            c0.seq(V.tensor_copy(endstep[:, :], endf[:, :]))
            V.tensor_copy(tile_row[:, :], tile_of[0:1, :]).then_inc(S_["path_dve"], 1)

            cq = Chain(dve, S_["q_dve"], QN)

            def q_turn(t, par, i):
                if not isinstance(t, int) or t < NT:
                    cq.start(t)
                    dve.wait_ge(S_[f"q_x{par}"], 16 * (i + 1))
                    wait(dve, S_["q_relu"], t - 1)
                    cq.seq(V.bn_stats(st[:, 0, :], xts[par]))
                    dve.sem_inc(S_["stats_made"], 1)
                    cq.seq(V.bn_aggr(mv[:, 0, :], st[:, 0, :]))
                    V.tensor_scalar(vr[:, 0:1], mv[:, 0, 1:2], EPS, None, ALU.add).then_inc(S_["q_rstd"], 1)
                    dve.wait_ge(S_["q_rstd"], 2 * t + 2)
                    cq.did(V.tensor_scalar(qns[par], xts[par], mv[:, 0, 0:1], vr[:, 1:2],
                                           ALU.subtract, ALU.mult))
                    cq.end()
                if not isinstance(t, int) or t >= 2:
                    dve.wait_ge(S_["q_mm"], t - 1)
                    wait(dve, S_[f"q_st{par}"], 32 * (i - 1))
                    V.tensor_copy(hv(kvos[par][:, D:KVW])[:, :, 0:HD],
                                  hv(bank[4 + par][:, 0:D])).then_inc(S_["q_vq"], 1)

            tiles(dve, q_turn)

            def fields(L, layer, B):
                b, par = B.n, B.par
                ch = Chain(dve, L["fld"], FLD)
                ch.start(b)
                dve.wait_ge(L["efl"][par], 32 * ST * (B.half + 1))
                wait(dve, L["smade"], b)
                wait(dve, L["oh_made"], 4 * (b - 1))
                wait(dve, L["ats_made"], b)
                wait(dve, L["bm_made"], b)
                dst = ef[:, par, :, 1]
                ch.did(V.scalar_tensor_tensor(
                    dloc[:, par, :].rearrange("p (s k) -> p s k", k=2),
                    tile_of[:, bass.ds(b * ST, ST)].unsqueeze(2).to_broadcast([P, ST, 2]), -float(P),
                    dst.rearrange("p (s k) -> p s k", k=2), ALU.mult, ALU.add))
                ch.seq(V.tensor_tensor(lk[:, 0, :], dst, ef[:, par, :, 2], ALU.is_equal))
                ch.did(V.tensor_scalar(msk[:, 0, :], dloc[:, par, :], 0.0, BIG, ALU.is_ge, ALU.mult))
                ch.did(V.tensor_scalar(msk[:, 1, :], dloc[:, par, :], float(P), BIG, ALU.is_lt, ALU.mult))
                ch.seq(V.tensor_scalar(lk[:, 1, :], lk[:, 0, :], -1.0, BIG, ALU.add, ALU.mult))
                V.tensor_copy(hc(arep[:, :]), lk[:, 1, :].unsqueeze(1).to_broadcast([P, H, CH])
                              ).then_inc(L["arep_made"], 1)
                ch.seq(V.tensor_tensor(msk[:, 2, :], msk[:, 0, :], msk[:, 1, :], ALU.add))
                ch.end()
                if layer == 0:
                    V.scalar_tensor_tensor(bm[:, :], msk[:, 2, :], -2 * BIG, ef[:, par, :, 3].bitcast(F32),
                                           ALU.add, ALU.add).then_inc(L["bm_made"], 1)
                else:
                    V.tensor_scalar(bm[:, :], msk[:, 2, :], -2 * BIG, None, ALU.add).then_inc(L["bm_made"], 1)

            def sames(L, B):
                wait(dve, L["accd"], (B.n - 1) * ST)
                V.tensor_copy(samec[:, B.par, :], same[:, bass.ds(B.n * ST, ST)]).then_inc(L["samec_made"], 1)

            def scores(L, layer, B):
                b = B.n
                g = rows[layer][B.slot]
                wait(dve, L["smade"], b)
                wait(dve, L["dmade"], b)
                if layer == 0:
                    def reduce(s):
                        dve.wait_ge(L["prodd"], b * ST + s + 1)
                        V.tensor_reduce(hc(sred[:, :])[:, :, 2 * s:2 * s + 2].rearrange("p h c -> p c h"),
                                        prod[:, s % 3, :, :].rearrange("p k (h w) -> p k h w", h=H), AXX,
                                        ALU.add).then_inc(L["redd"], 1)
                    for s in range(ST):
                        dve.wait_ge(L["gat"][B.slot][s], 32 * (B.lap + 1))
                        dve.wait_ge(L["qexp"], b * ST + s + 1)
                        if s >= 3:
                            dve.wait_ge(L["redd"], b * ST + s - 2)
                        V.tensor_tensor(prod[:, s % 3, :, :], g[:, 2 * s:2 * s + 2, 0:D],
                                        bank[2 + s % 2][:, :].rearrange("p (k n) -> p k n", k=2),
                                        ALU.mult).then_inc(L["prodd"], 1)
                        if s:
                            reduce(s - 1)
                    reduce(ST - 1)
                    dve.wait_ge(L["redd"], b * ST + ST)
                    V.scalar_tensor_tensor(hc(S[:, :]), hc(sred[:, :]), float(HD) ** -0.5,
                                           bm[:, :].unsqueeze(1).to_broadcast([P, H, CH]),
                                           ALU.mult, ALU.add).then_inc(L["smade"], 1)
                else:
                    dve.wait_ge(L["gat"][B.slot][0], 16 * CH * (B.lap + 1))
                    dve.wait_ge(L["qexp"], b * ST + ST)
                    V.tensor_tensor(hc(sred[:, :]), g[:, :, HV:FTW].rearrange("p c h -> p h c"),
                                    bank[2 + B.par][:, 0:P].rearrange("p (c h) -> p h c", h=H),
                                    ALU.add).then_inc(L["redd"], 1)
                    dve.wait_ge(L["redd"], 2 * b + 1)
                    V.scalar_tensor_tensor(prod[:, 0, 0, 0:P], sred[:, :], 0.2, sred[:, :],
                                           ALU.mult, ALU.max).then_inc(L["redd"], 1)
                    dve.wait_ge(L["redd"], 2 * b + 2)
                    V.tensor_tensor(hc(S[:, :]), hc(prod[:, 0, 0, 0:P]),
                                    bm[:, :].unsqueeze(1).to_broadcast([P, H, CH]),
                                    ALU.add).then_inc(L["smade"], 1)

            def weigh(L, layer, B, s):
                if s >= 4:
                    dve.wait_ge(L["agg"], B.n * ST + s - 3)
                val = rows[layer][B.slot][:, 2 * s:2 * s + 2, KVW - HV:KVW] if layer == 0 else \
                    rows[layer][B.slot][:, 2 * s:2 * s + 2, 0:HV]
                V.tensor_tensor(ev[:, s % 4, :, :].rearrange("p k (h w) -> p k h w", h=H),
                                val.rearrange("p k (h w) -> p k h w", h=H),
                                hc(ex[:, B.par, :])[:, :, 2 * s:2 * s + 2].rearrange("p h k -> p k h")
                                .unsqueeze(3).to_broadcast([P, 2, H, HD + 1]),
                                ALU.mult).then_inc(L["ev_made"], 1)

            def add(L, B, s):
                b, par = B.n, B.par
                dve.wait_ge(L["agg"], b * ST + s + 1)
                if s:
                    prev = acc[:, par, s - 1, :]
                    dve.wait_ge(L["accd"], b * ST + s)
                else:
                    prev = accr[:, :]
                    dve.wait_ge(L["resc"], b + 1)
                    dve.wait_ge(L["samec_made"], b + 1)
                V.scalar_tensor_tensor(acc[:, par, s, :], prev, samec[:, par, s:s + 1], bank[4 + s % 2][:, 0:HV],
                                       ALU.mult, ALU.add).then_inc(L["accd"], 1)

            def begin(L, B):
                b, par = B.n, B.par
                dve.wait_ge(L["ex_made"], b + 1)
                wait(dve, L["accd"], b * ST)
                wait(dve, L["acs"][par], 16 * ST * B.half)
                V.tensor_tensor(hv(accr[:, :]), hv(acc[:, 1 - par, ST - 1, :]),
                                rm[:, par, :].unsqueeze(2).to_broadcast([P, H, HD + 1]),
                                ALU.mult).then_inc(L["resc"], 1)

            def edge_phase(layer):
                L = L_[layer]

                def turn(B):
                    b = B.n
                    first = isinstance(b, int) and b == 0
                    last_ = isinstance(b, int) and b == NB - 1

                    def w(*ss):
                        if not first:
                            for s in ss:
                                weigh(L, layer, B.prev(), s)

                    def a(*ss):
                        if not first:
                            for s in ss:
                                add(L, B.prev(), s)

                    scores(L, layer, B)
                    if not first:
                        begin(L, B.prev())
                    w(0)
                    if not last_:
                        fields(L, layer, B.next())
                    w(1)
                    ch = Chain(dve, L["soft"], SOFT)
                    ch.start(b)
                    dve.wait_ge(L["s_tr"], b + 1)
                    dve.wait_ge(L["ats_made"], b + 1)
                    wait(dve, L["soft"], SOFT * b)
                    ST_ = bank[6][:, 0:P]
                    ch.did(V.tensor_tensor_scan(scan1[:, :], ats[:, 0:P], ST_, -BIG, ALU.add, ALU.max))
                    ch.did(V.tensor_tensor_scan(scan2[:, P - 1::-1], ats[:, P:0:-1], ST_[:, P - 1::-1], -BIG,
                                                ALU.add, ALU.max))
                    V.tensor_reduce(v4[:, 0:1], ats[:, 1:P], AXX, ALU.min).then_inc(L["v4_made"], 1)
                    V.tensor_copy(v4[:, 1:2], ats[:, 0:1]).then_inc(L["v4_made"], 1)
                    w(2)
                    a(0)
                    w(3)
                    a(1)
                    r = Chain(dve, L["row"], ROW)
                    r.start(b)
                    dve.wait_ge(L["rows_cp"], b + 1)
                    wait(dve, L["row"], ROW * b)
                    l_, f_, w_, a_ = [hc(rowS[:, k, :]) for k in range(4)]
                    r.did(V.tensor_tensor(hc(d0f[:, :])[:, :, 1:], w_[:, :, :CH - 1], a_[:, :, 1:], ALU.add))
                    r.did(V.tensor_tensor(hc(d1f[:, :])[:, :, 1:], l_[:, :, :CH - 1], a_[:, :, 1:], ALU.add))
                    r.did(V.tensor_tensor(hc(d1f[:, :])[:, :, 0], carry[:, :], a_[:, :, 0], ALU.add))
                    r.did(V.tensor_tensor(hc(d0b[:, :])[:, :, :CH - 1], w_[:, :, 1:], a_[:, :, 1:], ALU.add))
                    r.seq(V.tensor_tensor(hc(d1b[:, :])[:, :, :CH - 1], f_[:, :, 1:], a_[:, :, 1:], ALU.add))
                    r.did(V.tensor_tensor_scan(inr[:, :], d0f[:, :], d1f[:, :], -BIG, ALU.add, ALU.max))
                    r.seq(V.tensor_tensor_scan(outr[:, P - 1::-1], d0b[:, P - 1::-1], d1b[:, P - 1::-1], -BIG,
                                               ALU.add, ALU.max))
                    r.did(V.tensor_tensor(ct[:, 0, :], w_[:, :, CH - 1], hc(inr[:, :])[:, :, CH - 1], ALU.add))
                    r.seq(V.tensor_tensor(ct[:, 1, :], w_[:, :, 0], hc(outr[:, :])[:, :, 0], ALU.add))
                    r.did(V.tensor_tensor(carry[:, :], ct[:, 0, :], l_[:, :, CH - 1], ALU.max))
                    r.seq(V.tensor_tensor(ct[:, 2, :], ct[:, 1, :], f_[:, :, 0], ALU.max))
                    r.seq(V.tensor_tensor(ct[:, 3, :], ct[:, 2, :], hc(inr[:, :])[:, :, 0], ALU.max))
                    r.did(V.tensor_tensor(ct[:, 4, :], hc(d1f[:, :])[:, :, 0], ct[:, 3, :], ALU.subtract))
                    r.end()
                    a(2)
                    w(4)
                    a(3)
                    w(5)
                    dve.wait_ge(L["cols_cp"], b + 1)
                    ch.seq(V.tensor_tensor_scan(scan1[:, :], ats[:, 0:P], ST_, cols[:, 0:1], ALU.add, ALU.max))
                    ch.did(V.tensor_tensor_scan(scan2[:, P - 1::-1], ats[:, P:0:-1], scan1[:, P - 1::-1],
                                                cols[:, 1:2], ALU.add, ALU.max))
                    dve.wait_ge(L["oh0_made"], b + 1)
                    ch.seq(V.tensor_scalar(rt[:, :], bank[7][:, 8:8 + H], -1.0, oh0[:, B.par:B.par + 1],
                                           ALU.add, ALU.mult))
                    ch.seq(V.tensor_scalar(rm[:, B.par, :], rt[:, :], 1.0, None, ALU.add))
                    ch.end()
                    w(6)
                    a(4)
                    dve.wait_ge(L["m_tr"], b + 1)
                    V.tensor_tensor(df[:, :], S[:, :], bank[6][:, P:2 * P], ALU.subtract).then_inc(L["dmade"], 1)
                    w(7)
                    a(5, 6, 7)
                    if not last_:
                        sames(L, B.next())

                z = blk_at(0, layer)
                fields(L, layer, z)
                sames(L, z)
                blocks(dve, layer, turn)
                e = blk_at(NB - 1, layer)
                begin(L, e)
                for s in range(ST):
                    weigh(L, layer, e, s)
                    if s:
                        add(L, e, s - 1)
                add(L, e, ST - 1)

            edge_phase(0)

            dve.wait_ge(S_["m_w"], 16 * 15)
            c1 = Chain(dve, L_[1]["init"], 99)
            c1.start(0)
            c1.did(V.memset(carry[:, :], -BIG))
            c1.did(V.memset(fo[:, 0:HV], 1.0))
            c1.sync()
            first_acc = V.memset(acc[:, 1, ST - 1, :], 0.0)
            c1.seq(first_acc)

            def norm(ch, k, src, dst, var, rs, n):
                ch.seq(V.bn_stats(st[:, k, :], src))
                dve.sem_inc(S_["stats_made"], 1)
                ch.seq(V.bn_aggr(mv[:, k, :], st[:, k, :]))
                V.tensor_scalar(vr[:, 2 * k:2 * k + 1], mv[:, k, 1:2], EPS, None, ALU.add).then_inc(var, 1)
                dve.wait_ge(rs, n + 1)
                ch.seq(V.tensor_scalar(dst, src, mv[:, k, 0:1], vr[:, 2 * k + 1:2 * k + 2],
                                       ALU.subtract, ALU.mult))

            def m_turn(t):
                def on(k):
                    return not isinstance(t, int) or k <= t < NT + k
                if on(4):
                    u = t - 4
                    ch = Chain(dve, S_["m_dve4"], 5)
                    ch.start(u)
                    dve.wait_ge(S_["m_mm3"], u + 1)
                    wait(dve, S_["m_sft"], 32 * u)
                    feat = hv(fo[:, 0:HV])[:, :, 0:HD]
                    ch.seq(V.tensor_copy(feat, hv(bank[5][:, D:2 * D])))
                    ch.seq(V.tensor_tensor(hv(tmpel), feat, hv(v_al), ALU.mult))
                    ch.seq(V.tensor_reduce(fo[:, HV:FTW], hv(tmpel), AXX, ALU.add))
                    ch.seq(V.tensor_tensor(hv(tmpel), feat, hv(v_ar), ALU.mult))
                    ch.seq(V.tensor_reduce(ero, hv(tmpel), AXX, ALU.add))
                    ch.end()
                if on(3):
                    u = t - 3
                    ch = Chain(dve, S_["m_dve3"], 2)
                    ch.start(u)
                    dve.wait_ge(S_["m_mm2"], u + 1)
                    wait(dve, S_["m_sxh"], 16 * u)
                    ch.seq(V.tensor_tensor(hl, bank[4][:, D:2 * D], v_bl, ALU.add))
                    ch.seq(V.tensor_tensor(xh, xm, hl, ALU.add))
                    ch.end()
                if on(2):
                    u = t - 2
                    ch = Chain(dve, S_["m_dve2"], M2)
                    ch.start(u)
                    dve.wait_ge(S_["m_mm1"], u + 1)
                    ch.seq(V.tensor_tensor(z, bank[1][:, D:2 * D], v_b2, ALU.add))
                    ch.seq(V.tensor_tensor(z2, z, h1, ALU.add))
                    norm(ch, 2, z2, z, S_["m_var2"], S_["m_rs2"], u)
                    ch.seq(V.tensor_tensor(z2, z, v_g2, ALU.mult))
                    ch.seq(V.tensor_tensor(z, z2, v_b2n, ALU.add))
                    dve.wait_ge(S_["m_x"], 16 * (u + 1))
                    V.tensor_tensor(xm, xt, z, ALU.add).then_inc(S_["m_rdx"], 1)
                    dve.wait_ge(S_["m_rdx"], u + 1)
                    norm(ch, 3, xm, z2, S_["m_var3"], S_["m_rs3"], u)
                    ch.seq(V.tensor_scalar(h2, z2, 0.0, None, ALU.max))
                    ch.end()
                if on(1):
                    u = t - 1
                    ch = Chain(dve, S_["m_dve1"], M1)
                    ch.start(u)
                    dve.wait_ge(S_["m_mm0"], u + 1)
                    dve.wait_ge(S_["m_h"], 16 * (u + 1))
                    ch.seq(V.tensor_tensor(y, bank[0][:, D:2 * D], v_bp, ALU.add))
                    ch.seq(V.tensor_tensor(h1, y, ht, ALU.add))
                    norm(ch, 1, h1, y, S_["m_var1"], S_["m_rs1"], u)
                    ch.seq(V.tensor_tensor(h1, y, v_g1, ALU.mult))
                    ch.seq(V.tensor_tensor(h1, h1, v_b1n, ALU.add))
                    ch.end()
                if on(0):
                    ch = Chain(dve, S_["m_dve0"], M0)
                    ch.start(t)
                    dve.wait_ge(S_["m_acc"], 16 * (t + 1))
                    ch.seq(V.tensor_scalar(den[:, 0:H], hv(at_in)[:, :, HD], 1e-30, None, ALU.max))
                    ch.seq(V.reciprocal(den[:, H:2 * H], den[:, 0:H]))
                    V.tensor_tensor(hv(at), hv(at_in)[:, :, 0:HD],
                                    den[:, H:2 * H].unsqueeze(2).to_broadcast([P, H, HD]),
                                    ALU.mult).then_inc(S_["m_rdacc"], 1)
                    ch.end()

            for t in range(5):
                m_turn(t)
            with dve.Fori(5, NT) as t:
                m_turn(t)
            for t in range(NT, NT + 4):
                m_turn(t)

            edge_phase(1)

            dve.wait_ge(S_["m_w"], 16 * 16)
            cf = Chain(dve, S_["f_dve"], FIN)

            def f_turn(t, par, i):
                cf.start(t)
                dve.wait_ge(S_[f"f_acc{par}"], 16 * (i + 1))
                dve.wait_ge(S_[f"f_xh{par}"], 16 * (i + 1))
                wait(dve, S_[f"f_st{par}"], 16 * i)
                a, d, o = fin_a[par], fin_d[par], fin_o[par]
                cf.seq(V.tensor_scalar(d[:, 0:H], hv(fin_in[par])[:, :, HD], 1e-30, None, ALU.max))
                cf.seq(V.reciprocal(d[:, H:2 * H], d[:, 0:H]))
                cf.seq(V.tensor_tensor(hv(a), hv(fin_in[par])[:, :, 0:HD],
                                       d[:, H:2 * H].unsqueeze(2).to_broadcast([P, H, HD]), ALU.mult))
                cf.seq(V.tensor_tensor(o, a, v_gb, ALU.add))
                cf.seq(V.scalar_tensor_tensor(a, o, 0.01, o, ALU.mult, ALU.max))
                cf.seq(V.tensor_tensor(o, a, fin_xh[par], ALU.add))
                cf.end()

            f_turn(0, 0, 0)
            f_turn(1, 1, 0)
            with dve.Fori(1, NT // 2) as i:
                for par in range(2):
                    f_turn(2 * i + par, par, i)


_W = ["L0_gnn_Wq", "L0_gnn_Wk", "L0_gnn_Wv", "L0_gnn_Wp", "L0_gnn_bp", "L0_gnn_ln1_g", "L0_gnn_ln1_b",
      "L0_gnn_ln2_g", "L0_gnn_ln2_b", "L0_gnn_W1", "L0_gnn_b1", "L0_gnn_W2", "L0_gnn_b2",
      "L1_gnn_W_lin", "L1_gnn_b_lin", "L1_gnn_W_gat", "L1_gnn_attn_l", "L1_gnn_attn_r", "L1_gnn_gat_bias"]


def kernel(**inputs):
    import numpy as np
    import concourse.bacc as bacc
    from concourse.bass_utils import run_bass_kernel_spmd as run

    a = {k: np.ascontiguousarray(v) for k, v in inputs.items()}
    x = np.concatenate([a["x"], np.zeros((NPAD - N, D), np.float32)])
    pad = NSPAN * SPAN - E
    i32 = lambda n, v: np.full(n, v, np.int32)
    src = np.concatenate([a["src"], i32(pad + SPAN, 0)])
    dst = np.concatenate([a["dst"], i32(pad, NPAD - 1), i32(SPAN, NOWHERE)])
    prev = np.concatenate([i32(1, -1), dst[:-1]])
    bias = np.concatenate([a["edge_weight1"].reshape(-1).view(np.int32), i32(pad + SPAN, 0)])
    edges = np.stack([src, dst, prev, bias], -1).reshape(NSPAN + 1, 2, P, 4).transpose(0, 2, 1, 3)
    last = np.concatenate([dst[:NSPAN * SPAN].reshape(NSPAN, SPAN)[:, -1], i32(LC * P - NSPAN, 1 << 30)])
    arrays = {"x": x, "last": last, "edges": np.ascontiguousarray(edges.reshape(-1, 8))}
    arrays.update({n: a[n].reshape(-1) if a[n].shape == (H, HD) else a[n] for n in _W})
    nc = bacc.Bacc("TRN2", target_bir_lowering=False, num_devices=1)
    args = [nc.dram_tensor(f"in_{n}", v.shape, mybir.dt.from_np(v.dtype), kind="ExternalInput").ap()
            for n, v in arrays.items()]
    o = nc.dram_tensor("out_0", (N, D), F32, kind="ExternalOutput").ap()
    build(nc, *args, o)
    r = run(nc, [{f"in_{n}": v for n, v in arrays.items()}], core_ids=[0])
    return r.results[0]["out_0"]
```

```python
from contextlib import ExitStack

import concourse.bass as bass
from concourse import mybir

F32 = mybir.dt.float32
I32 = mybir.dt.int32
ALU = mybir.AluOpType
ACT = mybir.ActivationFunctionType
AXX = mybir.AxisListType.X

P = 128
N, D, H, E = 12500, 256, 8, 200000
HD = D // H
FFN = 4 * D
FC = FFN // P
NT = -(-N // P)
NPAD = NT * P
SPAN = 2 * P
NSPAN = -(-E // SPAN)
ST = 8
CH = 2 * ST
NB = -(-(NSPAN + NT) // ST)
NS = NB * ST
LC = -(-NSPAN // P)
HV = H * (HD + 1)
KVW = D + HV
FTW = HV + H
BIG = 1.0e30
EPS = 1e-5
NOWHERE = 1 << 20
RING = (2, 4)
assert NB % 2 == 0 and NB >= 6 and NS > NSPAN + NT - 1


class Chain:

    def __init__(self, eng, sem, per):
        self.eng, self.sem, self.per, self.k, self.n = eng, sem, per, 0, 0

    def start(self, n):
        self.k, self.n = 0, n

    def did(self, ins):
        ins.then_inc(self.sem, 1)
        self.k += 1

    def sync(self):
        self.eng.wait_ge(self.sem, self.n * self.per + self.k)

    def seq(self, ins):
        self.did(ins)
        self.sync()

    def end(self):
        assert self.k == self.per, (self.k, self.per)


class Blk:

    def __init__(self, n, quad, lap4, ring):
        self.n, self.quad, self.lap4, self.ring = n, quad, lap4, ring
        self.par, self.half = quad % 2, lap4 * 2 + quad // 2
        self.slot, self.lap = (self.par, self.half) if ring == 2 else (quad, lap4)

    def next(self):
        return Blk(self.n + 1, (self.quad + 1) % 4, self.lap4 + (self.quad + 1) // 4, self.ring)

    def prev(self):
        return Blk(self.n - 1, (self.quad - 1) % 4, self.lap4 - (1 if self.quad == 0 else 0), self.ring)


def blk_at(b, layer):
    return Blk(b, b % 4, b // 4, RING[layer])


def blocks(eng, layer, turn):
    whole = (NB - 2) // 4
    for b in range(4):
        turn(blk_at(b, layer))
    with eng.Fori(1, whole) as i:
        for k in range(4):
            turn(Blk(i * 4 + k, k, i, RING[layer]))
    for b in range(whole * 4, NB):
        turn(blk_at(b, layer))


def tiles(eng, turn):
    def at(t, quad, lap):
        turn(t, [(quad - k) % 4 for k in range(3)], [lap - (quad < k) for k in range(3)])
    for t in range(8):
        at(t, t % 4, t // 4)
    with eng.Fori(2, NT // 4) as i:
        for quad in range(4):
            at(4 * i + quad, quad, i)
    for t in range(NT // 4 * 4, NT + 2):
        at(t, t % 4, t // 4)


def m_turns(eng, turn):
    for t in range(6):
        turn(t)
    with eng.Fori(6, NT) as t:
        turn(t)
    for t in range(NT, NT + 4):
        turn(t)


def on(k, t):
    return not isinstance(t, int) or k <= t < NT + k


def wait(eng, sem, count):
    if isinstance(count, int) and count <= 0:
        return
    eng.wait_ge(sem, count)


def build(nc, x, last, edges, Wq, Wk, Wv, Wp, bp, g1, b1n, g2, b2n, W1, b1, W2, b2,
          Wl, bl, Wg, al, ar, gb, out):
    ctx = ExitStack()
    with ctx:
        def sb(name, shape, dt=F32):
            return ctx.enter_context(nc.sbuf_tensor(name, shape, dt))

        def sem(name):
            return ctx.enter_context(nc.semaphore(name))

        def dram(name, shape):
            return nc.dram_tensor(name, shape, F32, kind="Internal").ap()

        kv_tab = dram("kv_tab", (NPAD, KVW))
        q_tab = dram("q_tab", (NPAD, D))
        h_tab = dram("h_tab", (NPAD, D))
        ft_tab = dram("ft_tab", (NPAD, FTW))
        er_tab = dram("er_tab", (NPAD, H))
        xh_tab = dram("xh_tab", (NPAD, D))
        sums = dram("sums", (NS * P, HV))

        ident = sb("ident", [P, P])
        ones = sb("ones", [P, P])
        lane = sb("lane", [P, P])
        steps = sb("steps", [P, NS])
        spanid = sb("spanid", [P, LC])
        tile_of = sb("tile_of", [P, NS])
        same = sb("same", [P, NS])
        tile_row = sb("tile_row", [1, NS], I32)
        endstep = sb("endstep", [1, NT], I32)
        endf = sb("endf", [1, NT])
        last_i = sb("last_i", [P, LC], I32)
        last_t = sb("last_t", [P, LC], I32)
        last_f = sb("last_f", [P, LC])
        last_s = sb("last_s", [P, LC])
        mhalf = sb("mhalf", [P, 1])

        GW = max(RING[0] * CH * KVW, RING[1] * CH * FTW)
        Gf = sb("Gf", [P, GW])[:, :]
        rows = [[Gf[:, k * CH * w:(k + 1) * CH * w].rearrange("p (c w) -> p c w", c=CH) for k in range(n)]
                for n, w in ((RING[0], KVW), (RING[1], FTW))]
        ef = sb("ef", [P, 2, CH, 4], I32)
        qs = sb("qs", [P, 2, ST, D])
        oh = sb("oh", [P, 4, CH, P])
        oht = sb("oht", [P, 2, 4, P])
        oh0 = sb("oh0", [P, 2])
        prod = sb("prod", [P, 3, 2, D])
        absd = sb("absd", [P, 2, 4, P])
        ev = sb("ev", [P, 4, 2, HV])
        acc = sb("acc", [P, 2, ST, HV])
        accr = sb("accr", [P, HV])
        dloc = sb("dloc", [P, 2, CH])
        samec = sb("samec", [P, 2, ST])
        lk = sb("lk", [P, 2, CH])
        msk = sb("msk", [P, 3, CH])
        bm = sb("bm", [P, CH])
        arep = sb("arep", [P, P])
        ats = sb("ats", [P, P + 1])
        sred = sb("sred", [P, P])
        S = sb("S", [P, P])
        scan1 = sb("scan1", [P, P])
        scan2 = sb("scan2", [P, P])
        v4 = sb("v4", [P, 2])
        rowS = sb("rowS", [1, 4, P])
        d0f = sb("d0f", [1, P])
        d1f = sb("d1f", [1, P])
        d0b = sb("d0b", [1, P])
        d1b = sb("d1b", [1, P])
        inr = sb("inr", [1, P])
        outr = sb("outr", [1, P])
        carry = sb("carry", [1, H])
        ct = sb("ct", [1, 5, H])
        rexp = sb("rexp", [1, H])
        cols = sb("cols", [P, 2])
        rt = sb("rt", [P, H])
        rm = sb("rm", [P, 2, H])
        df = sb("df", [P, P])
        ex = sb("ex", [P, 2, P])

        bank = [ctx.enter_context(nc.psum_tensor(f"bank{i}", [P, 512], F32)) for i in range(8)]

        used = [0]

        def carve(n):
            a = used[0]
            used[0] += n
            assert used[0] <= GW
            return Gf[:, a:a + n]

        st = sb("st", [P, 4, 6])
        mv = sb("mv", [P, 4, 2])
        vr = sb("vr", [P, 8])

        w_v = carve(2 * D).rearrange("p (k n) -> p k n", k=2)
        w_kq = carve(4 * D).rearrange("p (k n) -> p k n", k=2)
        xts, hts, hTs, kvos, qos, qns = [[carve(w) for _ in range(4)] for w in (D, D, D, KVW, D, D)]

        used[0] = 0
        w_p = carve(2 * D).rearrange("p (k n) -> p k n", k=2)
        w_1 = carve(2 * FFN).rearrange("p (k n) -> p k n", k=2)
        w_2 = carve(FC * D).rearrange("p (k n) -> p k n", k=FC)
        w_l = carve(2 * D).rearrange("p (k n) -> p k n", k=2)
        w_ge = carve(2 * (D + 2 * H)).rearrange("p (k n) -> p k n", k=2)
        v_bp, v_g1, v_b1n, v_g2, v_b2n, v_b2, v_al, v_ar = [carve(D) for _ in range(8)]
        v_b1, v_bl = carve(FC), carve(2)
        xt, ht, xb, hb, h1b = [carve(D) for _ in range(5)]
        at_in, at, atT, den = carve(HV), carve(D), carve(D), carve(2 * H)
        y, y2, h1, h1T, gT = carve(D), carve(D), carve(D), carve(D), carve(FFN)
        z, z2, xm, h2, h2T, hlT, xh = [carve(D) for _ in range(7)]
        fo, ero, wtmp = carve(FTW), carve(H), carve(D)

        used[0] = 0
        v_gb = carve(D)
        fin_in, fin_xh = [[carve(w) for _ in range(4)] for w in (HV, D)]
        fin_a, fin_o, fin_d = [[carve(w) for _ in range(2)] for w in (D, D, 2 * H)]

        ohf = oh[:, :, :, :].rearrange("p a c n -> p (a c n)")
        qsf = qs[:, :, :, :].rearrange("p a s n -> p (a s n)")
        cmp_ = [(ohf if c < 4 else qsf)[:, (c % 4) * NS:(c % 4 + 1) * NS] for c in range(LC)]
        cmpe = [ev[:, :, :, :].rearrange("p a k n -> p (a k n)")[:, c * NT:(c + 1) * NT] for c in range(LC)]
        S_ = {}
        for name in """const_made gather_free stats_made setup_loaded path_dve path_pe w_loaded
            q_x0 q_x1 q_x2 q_x3 q_dve q_rstd q_relu q_tr q_hT q_mm q_ka q_st0 q_st1 q_st2 q_st3 q_vq
            m_w m_wge m_acc m_h m_x m_dve0 m_dve1 m_dve2 m_dve3 m_var1 m_var2 m_var3 m_rs1 m_rs2 m_rs3
            m_tr0 m_tr1 m_tr2 m_tr3 m_cp0 m_cp1 m_cp2 m_cp3 m_mm0 m_mm1 m_mm2 m_mm3 m_w1 m_gelu
            m_sxh m_sft m_rdacc m_fo m_xb m_hb m_h1b f_in0 f_in1 f_in2 f_in3 f_dve f_st0 f_st1""".split():
            S_[name] = sem(name)
        L_ = []
        for layer in range(2):
            d = {}
            for name in """fld samec_made ohd arep_made oh_made pat ats_made oht_tr oht_cp qexp prodd redd smade
                s_tr soft v4_made oh0_made rows_mm rows_cp row cols_mm cols_cp r_exp bm_made
                m_tr dmade ex_made ev_made agg accd resc init""".split():
                if name != "prodd" or layer == 0:
                    d[name] = sem(f"{name}_{layer}")
            d["efl"] = [sem(f"efl{layer}{p}") for p in range(2)]
            d["acs"] = [sem(f"acs{layer}{p}") for p in range(2)]
            d["gat"] = ([[sem(f"gat{p}_{s}") for s in range(ST)] for p in range(2)] if layer == 0
                        else [[sem(f"gath{k}")] for k in range(RING[1])])
            L_.append(d)

        FLD, SOFT, ROW = 6, 6, 13
        M0, M1, M2 = 2, 5, 8
        QN = 3
        FIN = 6
        block = ctx.enter_context(nc.Block())

        def hc(ap):
            return ap.rearrange("p (h c) -> p h c", h=H)

        def hv(ap):
            return ap.rearrange("p (h w) -> p h w", h=H)

        @block.sync
        def _(sp):
            sp.dma_start(last_i[:, :], last.rearrange("(p c) -> p c", c=LC)).then_inc(S_["setup_loaded"], 16)
            for w, src in ((w_v, Wv), (w_kq[:, :, 0:D], Wk), (w_kq[:, :, D:2 * D], Wq)):
                sp.dma_start(w, src.rearrange("(k p) n -> p k n", p=P)).then_inc(S_["w_loaded"], 16)

            def q_load(t, k):
                wait(sp, S_["q_dve"], QN * (t - 3))
                sp.dma_start(xts[k], x[bass.ds(t * P, P), :]).then_inc(S_[f"q_x{k}"], 16)

            def q_store(t, k):
                sp.wait_ge(S_["q_relu"], t + 1)
                sp.dma_start(h_tab[bass.ds(t * P, P), :], hts[k]).then_inc(S_[f"q_st{k}"], 16)
                sp.wait_ge(S_["q_vq"], t + 1)
                sp.wait_ge(S_["q_ka"], 2 * t + 2)
                sp.dma_start(kv_tab[bass.ds(t * P, P), :], kvos[k]).then_inc(S_[f"q_st{k}"], 16)
                sp.dma_start(q_tab[bass.ds(t * P, P), :], qos[k]).then_inc(S_[f"q_st{k}"], 16)

            def q_turn(t, k):
                if not isinstance(t, int) or t + 3 < NT:
                    q_load(t + 3, (k + 3) % 4)
                if not isinstance(t, int) or t >= 2:
                    q_store(t - 2, (k + 2) % 4)

            for t in range(3):
                q_load(t, t)
            for t in range(4):
                q_turn(t, t)
            with sp.Fori(1, (NT - 3) // 4) as i:
                for k in range(4):
                    q_turn(4 * i + k, k)
            for t in range((NT - 3) // 4 * 4, NT + 2):
                q_turn(t, t % 4)
            for k in range(4):
                sp.wait_ge(S_[f"q_st{k}"], 48 * len(range(k, NT, 4)))
            sp.wait_ge(S_["path_dve"], 1)

            def edge_loads(L, layer, B):
                wait(sp, L["smade"], B.n - 1)
                for s in range(ST):
                    step = B.n * ST + s
                    t = sp.value_load(tile_row[0:1, bass.ds(step, 1)], min_val=0, max_val=NT - 1)
                    m = nc.s_assert_within(sp.snap(step - t), 0, NSPAN,
                                           skip_runtime_bounds_check_because="step = span + tile")
                    sp.dma_start(ef[:, B.par, 2 * s:2 * s + 2, :],
                                 edges[bass.ds(m * P, P), :].rearrange("p (k f) -> p k f", f=4)
                                 ).then_inc(L["efl"][B.par], 16)
                    tab, w = (q_tab, D) if layer == 0 else (er_tab, H)
                    sp.dma_start(qs[:, B.par, s, 0:w], tab[bass.ds(t * P, P), :]).then_inc(L["efl"][B.par], 16)

            def edge_phase(layer):
                L = L_[layer]
                blocks(sp, layer, lambda B: edge_loads(L, layer, B))
                for par in range(2):
                    sp.wait_ge(L["acs"][par], 16 * ST * (NB // 2))

            edge_phase(0)

            for w, src in ((w_p, Wp), (w_1, W1), (w_2, W2), (w_l, Wl), (w_ge[:, :, 0:D], Wg)):
                sp.dma_start(w, src.rearrange("(k p) n -> p k n", p=P)).then_inc(S_["m_w"], 16)
            for v, src in ((v_bp, bp), (v_g1, g1), (v_b1n, b1n), (v_g2, g2), (v_b2n, b2n), (v_b2, b2),
                           (v_al, al), (v_ar, ar)):
                sp.dma_start(v, src.partition_broadcast(P)).then_inc(S_["m_w"], 16)
            for v, src in ((v_b1, b1), (v_bl, bl)):
                sp.dma_start(v, src.rearrange("(c p) -> p c", p=P),
                             allow_slow_non_contiguous=True).then_inc(S_["m_w"], 16)

            def m_turn(t):
                if not isinstance(t, int) or t < NT:
                    wait(sp, S_["m_rdacc"], t)
                    e = sp.value_load(endstep[0:1, bass.ds(t, 1)], min_val=0, max_val=NS - 1)
                    sp.dma_start(at_in, sums[bass.ds(e * P, P), :]).then_inc(S_["m_acc"], 16)
                    wait(sp, S_["m_hb"], t)
                    sp.dma_start(ht, h_tab[bass.ds(t * P, P), :]).then_inc(S_["m_h"], 16)
                if not isinstance(t, int) or 2 <= t <= NT + 1:
                    wait(sp, S_["m_xb"], t - 2)
                    sp.dma_start(xt, x[bass.ds((t - 2) * P, P), :]).then_inc(S_["m_x"], 16)
                if not isinstance(t, int) or t >= 4:
                    u = t - 4
                    sp.wait_ge(S_["m_dve3"], u + 1)
                    sp.dma_start(xh_tab[bass.ds(u * P, P), :], xh).then_inc(S_["m_sxh"], 16)
                    sp.wait_ge(S_["m_fo"], 3 * u + 3)
                    sp.dma_start(ft_tab[bass.ds(u * P, P), :], fo).then_inc(S_["m_sft"], 16)
                    sp.dma_start(er_tab[bass.ds(u * P, P), :], ero).then_inc(S_["m_sft"], 16)

            m_turns(sp, m_turn)
            sp.wait_ge(S_["m_sxh"], 16 * NT)
            sp.wait_ge(S_["m_sft"], 32 * NT)

            edge_phase(1)

            sp.dma_start(v_gb, gb.partition_broadcast(P)).then_inc(S_["m_w"], 16)

            def f_load(t, k):
                wait(sp, S_["f_dve"], FIN * (t - 3))
                e = sp.value_load(endstep[0:1, bass.ds(t, 1)], min_val=0, max_val=NS - 1)
                sp.dma_start(fin_in[k], sums[bass.ds(e * P, P), :]).then_inc(S_[f"f_in{k}"], 16)
                sp.dma_start(fin_xh[k], xh_tab[bass.ds(t * P, P), :]).then_inc(S_[f"f_in{k}"], 16)

            def f_turn(t, k):
                if not isinstance(t, int) or t + 3 < NT:
                    f_load(t + 3, (k + 3) % 4)
                rows = N - t * P if isinstance(t, int) and t == NT - 1 else P
                sp.wait_ge(S_["f_dve"], FIN * (t + 1))
                sp.dma_start(out[bass.ds(t * P, rows), :], fin_o[k % 2][0:rows, :]).then_inc(S_[f"f_st{k % 2}"], 16)

            for t in range(3):
                f_load(t, t)
            for t in range(4):
                f_turn(t, t)
            with sp.Fori(1, (NT - 3) // 4) as i:
                for k in range(4):
                    f_turn(4 * i + k, k)
            for t in range((NT - 3) // 4 * 4, NT):
                f_turn(t, t % 4)
            for par in range(2):
                sp.wait_ge(S_[f"f_st{par}"], 16 * (NT // 2))

        @block.gpsimd
        def _(pool):
            cm = S_["const_made"]
            pool.memset(ident[:, :], 0.0).then_inc(cm, 1)
            pool.memset(ones[:, :], 1.0).then_inc(cm, 1)
            pool.memset(mhalf[:, :], -0.5).then_inc(cm, 1)
            pool.wait_ge(cm, 3)
            pool.affine_select(out=ident[:, :], in_=ident[:, :], compare_op=ALU.not_equal, fill=1.0,
                               base=0, pattern=[[-1, P]], channel_multiplier=1).then_inc(cm, 1)
            pool.iota(lane[:, :], [[1, P]], base=0, channel_multiplier=0,
                      allow_small_or_imprecise_dtypes=True).then_inc(cm, 1)
            pool.iota(steps[:, :], [[1, NS]], base=0, channel_multiplier=0,
                      allow_small_or_imprecise_dtypes=True).then_inc(cm, 1)
            pool.iota(spanid[:, :], [[1, LC]], base=0, channel_multiplier=LC,
                      allow_small_or_imprecise_dtypes=True).then_inc(cm, 1)

            def rstd(k, ready, n, done):
                pool.wait_ge(ready, n + 1)
                pool.tensor_tensor(vr[:, 2 * k + 1:2 * k + 2], vr[:, 2 * k:2 * k + 1], mhalf[:, :],
                                   ALU.pow).then_inc(done, 1)

            pool.wait_ge(cm, 7)
            with pool.Fori(0, NT) as t:
                rstd(0, S_["q_rstd"], 2 * t, S_["q_rstd"])

            def edge_phase(layer):
                L = L_[layer]
                tab = (kv_tab, ft_tab)[layer]

                def turn(B):
                    pool.wait_ge(L["efl"][B.par], 32 * ST * (B.half + 1))
                    for c in range(CH):
                        free = (B.n - B.ring) * ST + c // 2 + 1
                        if c % 2 == 0 and not (isinstance(free, int) and free <= 0):
                            pool.wait_ge(L["ev_made"], free)
                            pool.sem_inc(S_["gather_free"], 1)
                        elif c == 0:
                            pool.sem_inc(S_["gather_free"], 1)
                        pool.indirect_dma_start(
                            out=rows[layer][B.slot][:, c, :], out_offset=None, in_=tab,
                            in_offset=bass.IndirectOffsetOnAxis(ap=ef[:, B.par, c, 0:1], axis=0),
                        ).then_inc(L["gat"][B.slot][c // 2 if layer == 0 else 0], 16)

                blocks(pool, layer, turn)

            edge_phase(0)

            pool.wait_ge(S_["m_w"], 16 * 15)

            def m_turn(t):
                if on(2, t):
                    pool.wait_ge(S_["m_dve1"], M1 * (t - 2) + M1)
                    wait(pool, S_["m_dve2"], M2 * (t - 3) + 1)
                    pool.tensor_tensor(h1b, h1, v_b2, ALU.add).then_inc(S_["m_h1b"], 1)
                for k, stage in ((2, 3), (3, 3), (1, 1)):
                    if on(stage, t):
                        rstd(k, S_[f"m_var{k}"], t - stage, S_[f"m_rs{k}"])
                if on(2, t):
                    pool.wait_ge(S_["m_x"], 16 * (t - 1))
                    wait(pool, S_["m_dve2"], M2 * (t - 3) + 5)
                    pool.tensor_tensor(xb, xt, v_b2n, ALU.add).then_inc(S_["m_xb"], 1)
                if on(0, t):
                    pool.wait_ge(S_["m_h"], 16 * (t + 1))
                    wait(pool, S_["m_dve1"], M1 * (t - 1) + 1)
                    pool.tensor_tensor(hb, ht, v_bp, ALU.add).then_inc(S_["m_hb"], 1)

            m_turns(pool, m_turn)
            edge_phase(1)

        @block.scalar
        def _(act):
            def copy(o, i_, s):
                act.activation(o, i_, ACT.Copy).then_inc(s, 1)

            act.wait_ge(S_["const_made"], 7)

            def q_turn(t, slots, laps):
                a, b, c = slots
                if not isinstance(t, int) or t < NT:
                    act.wait_ge(S_["q_dve"], QN * (t + 1))
                    wait(act, S_[f"q_st{a}"], 48 * laps[0])
                    act.activation(hts[a], qns[a], ACT.Relu).then_inc(S_["q_relu"], 1)
                if not isinstance(t, int) or 1 <= t <= NT:
                    act.wait_ge(S_["q_tr"], t)
                    wait(act, S_["q_mm"], t - 4)
                    copy(hTs[b], bank[b % 2][:, 0:D], S_["q_hT"])
                if not isinstance(t, int) or t >= 2:
                    act.wait_ge(S_["q_mm"], t - 1)
                    wait(act, S_[f"q_st{c}"], 48 * laps[2])
                    copy(kvos[c][:, 0:D], bank[2 + c % 2][:, 0:D], S_["q_ka"])
                    copy(qos[c], bank[2 + c % 2][:, D:2 * D], S_["q_ka"])

            tiles(act, q_turn)

            def onehots(L, B, g):
                n = B.n * 4 + g
                act.wait_ge(L["fld"], FLD * (B.n + 1))
                wait(act, L["agg"], (B.n - 4) * ST + 2 * g + 2)
                wait(act, L["oh_made"], n - 1)
                for k in range(4):
                    act.activation(absd[:, g % 2, k, :], lane[:, :], ACT.Abs, scale=-1.0,
                                   bias=dloc[:, B.par, 4 * g + k:4 * g + k + 1]).then_inc(L["ohd"], 1)
                act.wait_ge(L["ohd"], 4 * n + 4)
                act.activation(oh[:, B.quad, 4 * g:4 * g + 4, :].rearrange("p c n -> p (c n)"),
                               absd[:, g % 2, :, :].rearrange("p c n -> p (c n)"), ACT.Relu, scale=-1.0,
                               bias=ones[:, 0:1]).then_inc(L["oh_made"], 1)

            def turned(L, B, g):
                act.wait_ge(L["oht_tr"], B.n * 4 + g + 1)
                wait(act, L["qexp"], B.n * ST + 2 * g - 2)
                if g == 2:
                    act.wait_ge(L["oh0_made"], B.n + 1)
                copy(oht[:, g % 2, :, :].rearrange("p c n -> p (c n)"), bank[g % 2][:, :], L["oht_cp"])
                if g == 0:
                    act.wait_ge(L["oht_cp"], B.n * 4 + 1)
                    wait(act, L["soft"], SOFT * (B.n - 1))
                    copy(oh0[:, B.par:B.par + 1], oht[:, 0, 0, 0:1], L["oh0_made"])

            def edge_phase(layer):
                L = L_[layer]

                def sum_store(B, s):
                    act.wait_ge(L["accd"], B.n * ST + s + 1)
                    act.dma_start(sums[bass.ds((B.n * ST + s) * P, P), :],
                                  acc[:, B.par, s, :]).then_inc(L["acs"][B.par], 16)

                def turn(B):
                    b = B.n
                    nx = None if isinstance(b, int) and b == NB - 1 else B.next()

                    def stored(back, *ss):
                        if not (isinstance(b, int) and b < back):
                            for s in ss:
                                sum_store(B.prev() if back == 1 else B.prev().prev(), s)

                    if layer == 0:
                        turned(L, B, 3)
                    act.wait_ge(L["pat"], b + 1)
                    wait(act, L["soft"], SOFT * b)
                    copy(ats[:, 0:P], bank[7][:, 0:P], L["ats_made"])
                    stored(2, ST - 2, ST - 1)
                    if nx:
                        onehots(L, nx, 0)
                    act.wait_ge(L["rows_mm"], b + 1)
                    copy(rowS[:, :, :].rearrange("p q n -> p (q n)"), bank[7][0:1, :], L["rows_cp"])
                    if nx:
                        onehots(L, nx, 1)
                        turned(L, nx, 0)
                        onehots(L, nx, 2)
                    act.wait_ge(L["row"], ROW * b + ROW)
                    act.activation(rexp[:, :], ct[:, 4, :], ACT.Exp).then_inc(L["r_exp"], 1)
                    act.wait_ge(L["cols_mm"], b + 1)
                    copy(cols[:, :], bank[7][:, 0:2], L["cols_cp"])
                    if nx:
                        turned(L, nx, 1)
                        onehots(L, nx, 3)
                        turned(L, nx, 2)
                    act.wait_ge(L["dmade"], b + 1)
                    act.activation(ex[:, B.par, :], df[:, :], ACT.Exp).then_inc(L["ex_made"], 1)
                    if nx and layer == 1:
                        turned(L, nx, 3)
                    stored(1, *range(ST - 2))

                z = blk_at(0, layer)
                for g in range(4):
                    onehots(L, z, g)
                for g in range(4 if layer == 1 else 3):
                    turned(L, z, g)
                blocks(act, layer, turn)
                sum_store(blk_at(NB - 2, layer), ST - 2)
                sum_store(blk_at(NB - 2, layer), ST - 1)
                for s in range(ST):
                    sum_store(blk_at(NB - 1, layer), s)

            edge_phase(0)

            act.wait_ge(S_["m_w"], 16 * 15)

            def m_turn(t):
                if on(2, t):
                    act.wait_ge(S_["m_tr1"], t - 1)
                    copy(h1T, bank[4][:, 0:D], S_["m_cp1"])
                if on(4, t):
                    u = t - 4
                    act.wait_ge(S_["m_mm3"], u + 1)
                    wait(act, S_["m_sft"], 32 * u)
                    copy(hv(fo[:, 0:HV])[:, :, 0:HD], hv(bank[7][:, 0:D]), S_["m_fo"])
                    copy(fo[:, HV:FTW], bank[7][:, D:D + H], S_["m_fo"])
                    copy(ero, bank[7][:, D + H:D + 2 * H], S_["m_fo"])
                if on(2, t):
                    u = t - 2
                    for f in range(FC):
                        if f % 4 == 0:
                            act.wait_ge(S_["m_w1"], 2 * u + f // 4 + 1)
                        act.activation(gT[:, f * P:(f + 1) * P], bank[2 + f // 4][:, (f % 4) * P:(f % 4 + 1) * P],
                                       ACT.Gelu, bias=v_b1[:, f:f + 1]).then_inc(S_["m_gelu"], 1)
                if on(0, t):
                    act.wait_ge(S_["m_tr0"], t + 1)
                    copy(atT, bank[4][:, 0:D], S_["m_cp0"])
                if on(3, t):
                    u = t - 3
                    act.wait_ge(S_["m_tr2"], u + 1)
                    act.activation(h2T, bank[5][:, 0:D], ACT.Relu).then_inc(S_["m_cp2"], 1)
                    act.wait_ge(S_["m_mm2"], u + 1)
                    for c in range(2):
                        act.activation(hlT[:, c * P:(c + 1) * P], bank[6][:, c * P:(c + 1) * P], ACT.Identity,
                                       bias=v_bl[:, c:c + 1]).then_inc(S_["m_cp3"], 1)

            m_turns(act, m_turn)
            edge_phase(1)

        @block.tensor
        def _(pe):
            def mm(o, a, r, first=True, end=True):
                return nc.tensor.matmul(o, a, r, start=first, stop=end)

            def tr(o, i_):
                return nc.tensor.transpose(o, i_, ident[:, :])

            pe.wait_ge(S_["const_made"], 7)
            pe.wait_ge(S_["path_pe"], 2 * LC)
            half = NS // 2
            for c in range(LC):
                for k in range(2):
                    mm(bank[4 + k][:, 0:half], ones[:, :], cmp_[c][:, k * half:(k + 1) * half],
                       c == 0, c == LC - 1)
                m = mm(bank[6][:, 0:NT], ones[:, :], cmpe[c], c == 0, c == LC - 1)
            m.then_inc(S_["path_pe"], 1)

            pe.wait_ge(S_["w_loaded"], 48)

            def q_turn(t, slots, laps):
                _, b, c = slots
                if not isinstance(t, int) or 1 <= t <= NT:
                    pe.wait_ge(S_["q_relu"], t)
                    wait(pe, S_["q_hT"], t - 2)
                    tr(bank[b % 2][:, 0:P], hts[b][:, 0:P])
                    tr(bank[b % 2][:, P:D], hts[b][:, P:D]).then_inc(S_["q_tr"], 1)
                if not isinstance(t, int) or t >= 2:
                    pe.wait_ge(S_["q_hT"], t - 1)
                    wait(pe, S_["q_vq"], t - 3)
                    wait(pe, S_["q_ka"], 2 * (t - 3))
                    for k in range(2):
                        mm(bank[2 + c % 2][:, :], hTs[c][:, k * P:(k + 1) * P], w_kq[:, k, :], k == 0, k == 1)
                    for k in range(2):
                        m = mm(bank[4 + c % 2][:, 0:D], hTs[c][:, k * P:(k + 1) * P], w_v[:, k, :], k == 0, k == 1)
                    m.then_inc(S_["q_mm"], 1)

            tiles(pe, q_turn)

            def turns(L, B, g):
                pe.wait_ge(L["oh_made"], B.n * 4 + g + 1)
                wait(pe, L["oht_cp"], B.n * 4 + g - 1)
                for k in range(4):
                    m = tr(bank[g % 2][:, k * P:(k + 1) * P], oh[:, B.quad, 4 * g + k, :])
                m.then_inc(L["oht_tr"], 1)

            def spread(L, layer, B, s):
                if s == 0:
                    pe.wait_ge(L["efl"][B.par], 32 * ST * (B.half + 1))
                if s % 2 == 0:
                    pe.wait_ge(L["oht_cp"], B.n * 4 + s // 2 + 1)
                if layer == 0:
                    wait(pe, L["prodd"], B.n * ST + s - 1)
                elif s == 0:
                    wait(pe, L["smade"], B.n - 1)
                for k in range(2):
                    a = oht[:, (s // 2) % 2, 2 * (s % 2) + k, :]
                    if layer == 0:
                        m = mm(bank[2 + s % 2][:, k * D:(k + 1) * D], a, qs[:, B.par, s, :])
                    else:
                        c = 2 * s + k
                        m = mm(bank[2 + B.par][:, c * H:(c + 1) * H], a, qs[:, B.par, s, 0:H])
                m.then_inc(L["qexp"], 1)

            def agg(L, B, s):
                pe.wait_ge(L["ev_made"], B.n * ST + s + 1)
                wait(pe, L["accd"], B.n * ST + s - 1)
                o = bank[4 + s % 2][:, 0:HV]
                mm(o, oh[:, B.quad, 2 * s, :], ev[:, s % 4, 0, :], True, False)
                mm(o, oh[:, B.quad, 2 * s + 1, :], ev[:, s % 4, 1, :], False, True).then_inc(L["agg"], 1)

            def edge_phase(layer):
                L = L_[layer]

                def turn(B):
                    b = B.n
                    first = isinstance(b, int) and b == 0
                    last_ = isinstance(b, int) and b == NB - 1

                    def aggs(*ss):
                        if not first:
                            for s in ss:
                                agg(L, B.prev(), s)

                    pe.wait_ge(L["arep_made"], b + 1)
                    wait(pe, L["ats_made"], b)
                    wait(pe, L["soft"], SOFT * b)
                    tr(bank[7][:, 0:P], arep[:, :]).then_inc(L["pat"], 1)
                    if layer == 0:
                        for s in range(2, ST):
                            spread(L, layer, B, s)
                    pe.wait_ge(L["smade"], b + 1)
                    tr(bank[6][:, 0:P], S[:, :]).then_inc(L["s_tr"], 1)
                    aggs(0)
                    pe.wait_ge(L["v4_made"], 2 * b + 2)
                    pe.wait_ge(L["soft"], SOFT * b + 2)
                    for q, v in enumerate((scan1[:, P - 1:P], scan2[:, 0:1], v4[:, 0:1], v4[:, 1:2])):
                        m = mm(bank[7][0:1, q * P:(q + 1) * P], v, ident[:, :])
                    m.then_inc(L["rows_mm"], 1)
                    nx = None if last_ else B.next()
                    aggs(1)
                    if nx:
                        turns(L, nx, 0)
                    aggs(2, 3)
                    if nx:
                        turns(L, nx, 1)
                        spread(L, layer, nx, 0)
                        spread(L, layer, nx, 1)
                    pe.wait_ge(L["row"], ROW * b + ROW)
                    pe.wait_ge(L["r_exp"], b + 1)
                    mm(bank[7][:, 0:1], inr[0:1, :], ones[0:1, 0:1])
                    mm(bank[7][:, 1:2], outr[0:1, :], ones[0:1, 0:1])
                    mm(bank[7][:, 8:8 + H], ones[0:1, :], rexp[0:1, :]).then_inc(L["cols_mm"], 1)
                    aggs(4)
                    pe.wait_ge(L["soft"], SOFT * b + 4)
                    tr(bank[6][:, P:2 * P], scan2[:, :]).then_inc(L["m_tr"], 1)
                    if nx:
                        turns(L, nx, 2)
                    aggs(5)
                    if nx and layer == 1:
                        spread(L, layer, nx, 2)
                        spread(L, layer, nx, 3)
                    if nx:
                        turns(L, nx, 3)
                    aggs(6)
                    if nx and layer == 1:
                        for s in range(4, ST):
                            spread(L, layer, nx, s)
                    aggs(7)

                z = blk_at(0, layer)
                for g in range(4):
                    turns(L, z, g)
                    if g < 1 or layer == 1:
                        spread(L, layer, z, 2 * g)
                        spread(L, layer, z, 2 * g + 1)
                blocks(pe, layer, turn)
                for s in range(ST):
                    agg(L, blk_at(NB - 1, layer), s)

            edge_phase(0)
            pe.wait_ge(S_["m_w"], 16 * 15)
            pe.wait_ge(S_["m_wge"], 1)

            def m_turn(t):
                def turned(b, at_, src, done):
                    tr(bank[b][:, at_:at_ + P], src[:, 0:P])
                    tr(bank[b][:, at_ + P:at_ + D], src[:, P:D]).then_inc(done, 1)

                def product(o, a, w, done):
                    for c in range(2):
                        m = mm(o, a[:, c * P:(c + 1) * P], w[:, c, :], c == 0, c == 1)
                    m.then_inc(done, 1)

                if on(2, t):
                    pe.wait_ge(S_["m_dve1"], M1 * (t - 2) + M1)
                    turned(4, 0, h1, S_["m_tr1"])
                if on(4, t):
                    u = t - 4
                    pe.wait_ge(S_["m_cp3"], 2 * u + 2)
                    turned(5, D, hlT, S_["m_tr3"])
                    wait(pe, S_["m_fo"], 3 * u)
                    product(bank[7][:, 0:D + 2 * H], hlT, w_ge, S_["m_mm3"])
                if on(2, t):
                    u = t - 2
                    pe.wait_ge(S_["m_cp1"], u + 1)
                    for f in range(FC):
                        for c in range(2):
                            m = mm(bank[2 + f // 4][:, (f % 4) * P:(f % 4 + 1) * P],
                                   w_1[:, c, f * P:(f + 1) * P], h1T[:, c * P:(c + 1) * P], c == 0, c == 1)
                        if f % 4 == 3:
                            m.then_inc(S_["m_w1"], 1)
                if on(0, t):
                    pe.wait_ge(S_["m_rdacc"], t + 1)
                    turned(4, 0, at, S_["m_tr0"])
                if on(2, t):
                    wait(pe, S_["m_dve2"], M2 * (u - 1) + 1)
                    for f in range(FC):
                        pe.wait_ge(S_["m_gelu"], FC * u + f + 1)
                        m = mm(bank[1][:, 0:D], gT[:, f * P:(f + 1) * P], w_2[:, f, :], f == 0, f == FC - 1)
                    m.then_inc(S_["m_mm1"], 1)
                if on(3, t):
                    pe.wait_ge(S_["m_dve2"], M2 * (t - 3) + M2)
                    turned(5, 0, h2, S_["m_tr2"])
                if on(0, t):
                    pe.wait_ge(S_["m_cp0"], t + 1)
                    wait(pe, S_["m_dve1"], M1 * (t - 1) + 1)
                    product(bank[0][:, 0:D], atT, w_p, S_["m_mm0"])
                if on(3, t):
                    pe.wait_ge(S_["m_cp2"], t - 2)
                    for k in range(2):
                        for c in range(2):
                            m = mm(bank[6][:, k * P:(k + 1) * P], w_l[:, c, k * P:(k + 1) * P],
                                   h2T[:, c * P:(c + 1) * P], c == 0, c == 1)
                    m.then_inc(S_["m_mm2"], 1)

            m_turns(pe, m_turn)
            edge_phase(1)

        @block.vector
        def _(dve):
            V = nc.vector
            dve.wait_ge(S_["const_made"], 7)
            dve.wait_ge(S_["setup_loaded"], 16)
            c0 = Chain(dve, L_[0]["init"], 99)
            c0.start(0)
            c0.did(V.memset(ats[:, P:P + 1], 0.0))
            c0.did(V.memset(d0f[:, :], -BIG))
            c0.did(V.memset(d0b[:, :], -BIG))
            c0.did(V.memset(d1b[:, :], -BIG))
            c0.did(V.memset(carry[:, :], -BIG))
            c0.did(V.memset(acc[:, 1, ST - 1, :], 0.0))
            for kvo in kvos:
                c0.did(V.memset(kvo[:, D:KVW], 1.0))
            c0.seq(V.tensor_scalar(last_t[:, :], last_i[:, :], 7, None, ALU.logical_shift_right))
            c0.seq(V.tensor_copy(last_f[:, :], last_t[:, :]))
            c0.seq(V.tensor_tensor(last_s[:, :], last_f[:, :], spanid[:, :], ALU.add))
            for c in range(LC):
                V.tensor_scalar(cmp_[c], steps[:, :], last_s[:, c:c + 1], None,
                                ALU.is_gt).then_inc(S_["path_pe"], 1)
                V.tensor_scalar(cmpe[c], steps[:, 0:NT], last_f[:, c:c + 1], None,
                                ALU.is_ge).then_inc(S_["path_pe"], 1)
            dve.wait_ge(S_["path_pe"], 2 * LC + 1)
            half = NS // 2
            for k in range(2):
                c0.seq(V.tensor_tensor(tile_of[:, k * half:(k + 1) * half], steps[:, k * half:(k + 1) * half],
                                       bank[4 + k][:, 0:half], ALU.subtract))
            c0.seq(V.memset(same[:, 0:1], 0.0))
            c0.seq(V.tensor_tensor(same[:, 1:NS], tile_of[:, 1:NS], tile_of[:, 0:NS - 1], ALU.is_equal))
            c0.seq(V.tensor_tensor(endf[:, :], bank[6][0:1, 0:NT], steps[0:1, 0:NT], ALU.add))
            c0.seq(V.tensor_copy(endstep[:, :], endf[:, :]))
            V.tensor_copy(tile_row[:, :], tile_of[0:1, :]).then_inc(S_["path_dve"], 1)

            cq = Chain(dve, S_["q_dve"], QN)

            def q_turn(t, slots, laps):
                if not isinstance(t, int) or t < NT:
                    a = slots[0]
                    cq.start(t)
                    dve.wait_ge(S_[f"q_x{a}"], 16 * (laps[0] + 1))
                    wait(dve, S_["q_relu"], t - 3)
                    cq.seq(V.bn_stats(st[:, 0, :], xts[a]))
                    dve.sem_inc(S_["stats_made"], 1)
                    cq.seq(V.bn_aggr(mv[:, 0, :], st[:, 0, :]))
                    V.tensor_scalar(vr[:, 0:1], mv[:, 0, 1:2], EPS, None, ALU.add).then_inc(S_["q_rstd"], 1)
                    dve.wait_ge(S_["q_rstd"], 2 * t + 2)
                    cq.did(V.tensor_scalar(qns[a], xts[a], mv[:, 0, 0:1], vr[:, 1:2],
                                           ALU.subtract, ALU.mult))
                    cq.end()
                if not isinstance(t, int) or t >= 2:
                    dve.wait_ge(S_["q_mm"], t - 1)
                    c = slots[2]
                    wait(dve, S_[f"q_st{c}"], 48 * laps[2])
                    V.tensor_copy(hv(kvos[c][:, D:KVW])[:, :, 0:HD],
                                  hv(bank[4 + c % 2][:, 0:D])).then_inc(S_["q_vq"], 1)

            tiles(dve, q_turn)

            def fields(L, layer, B):
                b, par = B.n, B.par
                ch = Chain(dve, L["fld"], FLD)
                ch.start(b)
                dve.wait_ge(L["efl"][par], 32 * ST * (B.half + 1))
                wait(dve, L["smade"], b)
                wait(dve, L["oh_made"], 4 * (b - 1))
                wait(dve, L["ats_made"], b)
                wait(dve, L["bm_made"], b)
                dst = ef[:, par, :, 1]
                ch.did(V.scalar_tensor_tensor(
                    dloc[:, par, :].rearrange("p (s k) -> p s k", k=2),
                    tile_of[:, bass.ds(b * ST, ST)].unsqueeze(2).to_broadcast([P, ST, 2]), -float(P),
                    dst.rearrange("p (s k) -> p s k", k=2), ALU.mult, ALU.add))
                ch.seq(V.tensor_tensor(lk[:, 0, :], dst, ef[:, par, :, 2], ALU.is_equal))
                ch.did(V.tensor_scalar(msk[:, 0, :], dloc[:, par, :], 0.0, BIG, ALU.is_ge, ALU.mult))
                ch.did(V.tensor_scalar(msk[:, 1, :], dloc[:, par, :], float(P), BIG, ALU.is_lt, ALU.mult))
                ch.seq(V.tensor_scalar(lk[:, 1, :], lk[:, 0, :], -1.0, BIG, ALU.add, ALU.mult))
                V.tensor_copy(hc(arep[:, :]), lk[:, 1, :].unsqueeze(1).to_broadcast([P, H, CH])
                              ).then_inc(L["arep_made"], 1)
                ch.seq(V.tensor_tensor(msk[:, 2, :], msk[:, 0, :], msk[:, 1, :], ALU.add))
                ch.end()
                if layer == 0:
                    V.scalar_tensor_tensor(bm[:, :], msk[:, 2, :], -2 * BIG, ef[:, par, :, 3].bitcast(F32),
                                           ALU.add, ALU.add).then_inc(L["bm_made"], 1)
                else:
                    V.tensor_scalar(bm[:, :], msk[:, 2, :], -2 * BIG, None, ALU.add).then_inc(L["bm_made"], 1)

            def sames(L, B):
                wait(dve, L["accd"], (B.n - 1) * ST)
                V.tensor_copy(samec[:, B.par, :], same[:, bass.ds(B.n * ST, ST)]).then_inc(L["samec_made"], 1)

            def scores(L, layer, B, late):
                b = B.n
                g = rows[layer][B.slot]
                wait(dve, L["smade"], b)
                wait(dve, L["dmade"], b)
                if layer == 0:
                    def reduce(s):
                        dve.wait_ge(L["prodd"], b * ST + s + 1)
                        V.tensor_reduce(hc(sred[:, :])[:, :, 2 * s:2 * s + 2].rearrange("p h c -> p c h"),
                                        prod[:, s % 3, :, :].rearrange("p k (h w) -> p k h w", h=H), AXX,
                                        ALU.add).then_inc(L["redd"], 1)
                    for s in range(ST):
                        dve.wait_ge(L["gat"][B.slot][s], 32 * (B.lap + 1))
                        dve.wait_ge(L["qexp"], b * ST + s + 1)
                        if s >= 3:
                            dve.wait_ge(L["redd"], b * ST + s - 2)
                        V.tensor_tensor(prod[:, s % 3, :, :], g[:, 2 * s:2 * s + 2, 0:D],
                                        bank[2 + s % 2][:, :].rearrange("p (k n) -> p k n", k=2),
                                        ALU.mult).then_inc(L["prodd"], 1)
                        if s:
                            reduce(s - 1)
                        if s == 1:
                            late()
                    reduce(ST - 1)
                    dve.wait_ge(L["redd"], b * ST + ST)
                    V.scalar_tensor_tensor(hc(S[:, :]), hc(sred[:, :]), float(HD) ** -0.5,
                                           bm[:, :].unsqueeze(1).to_broadcast([P, H, CH]),
                                           ALU.mult, ALU.add).then_inc(L["smade"], 1)
                else:
                    dve.wait_ge(L["gat"][B.slot][0], 16 * CH * (B.lap + 1))
                    dve.wait_ge(L["qexp"], b * ST + ST)
                    V.tensor_tensor(hc(sred[:, :]), g[:, :, HV:FTW].rearrange("p c h -> p h c"),
                                    bank[2 + B.par][:, 0:P].rearrange("p (c h) -> p h c", h=H),
                                    ALU.add).then_inc(L["redd"], 1)
                    late()
                    dve.wait_ge(L["redd"], 2 * b + 1)
                    V.scalar_tensor_tensor(prod[:, 0, 0, 0:P], sred[:, :], 0.2, sred[:, :],
                                           ALU.mult, ALU.max).then_inc(L["redd"], 1)
                    dve.wait_ge(L["redd"], 2 * b + 2)
                    V.tensor_tensor(hc(S[:, :]), hc(prod[:, 0, 0, 0:P]),
                                    bm[:, :].unsqueeze(1).to_broadcast([P, H, CH]),
                                    ALU.add).then_inc(L["smade"], 1)

            def weigh(L, layer, B, s):
                if s >= 4:
                    dve.wait_ge(L["agg"], B.n * ST + s - 3)
                val = rows[layer][B.slot][:, 2 * s:2 * s + 2, KVW - HV:KVW] if layer == 0 else \
                    rows[layer][B.slot][:, 2 * s:2 * s + 2, 0:HV]
                V.tensor_tensor(ev[:, s % 4, :, :].rearrange("p k (h w) -> p k h w", h=H),
                                val.rearrange("p k (h w) -> p k h w", h=H),
                                hc(ex[:, B.par, :])[:, :, 2 * s:2 * s + 2].rearrange("p h k -> p k h")
                                .unsqueeze(3).to_broadcast([P, 2, H, HD + 1]),
                                ALU.mult).then_inc(L["ev_made"], 1)

            def add(L, B, s):
                b, par = B.n, B.par
                dve.wait_ge(L["agg"], b * ST + s + 1)
                if s:
                    prev = acc[:, par, s - 1, :]
                    dve.wait_ge(L["accd"], b * ST + s)
                else:
                    prev = accr[:, :]
                    dve.wait_ge(L["resc"], b + 1)
                    dve.wait_ge(L["samec_made"], b + 1)
                V.scalar_tensor_tensor(acc[:, par, s, :], prev, samec[:, par, s:s + 1], bank[4 + s % 2][:, 0:HV],
                                       ALU.mult, ALU.add).then_inc(L["accd"], 1)

            def begin(L, B):
                b, par = B.n, B.par
                dve.wait_ge(L["ex_made"], b + 1)
                wait(dve, L["accd"], b * ST)
                wait(dve, L["acs"][par], 16 * ST * B.half)
                V.tensor_tensor(hv(accr[:, :]), hv(acc[:, 1 - par, ST - 1, :]),
                                rm[:, par, :].unsqueeze(2).to_broadcast([P, H, HD + 1]),
                                ALU.mult).then_inc(L["resc"], 1)

            def edge_phase(layer):
                L = L_[layer]

                def turn(B):
                    b = B.n
                    first = isinstance(b, int) and b == 0
                    last_ = isinstance(b, int) and b == NB - 1

                    def w(*ss):
                        if not first:
                            for s in ss:
                                weigh(L, layer, B.prev(), s)

                    def a(*ss):
                        if not first:
                            for s in ss:
                                add(L, B.prev(), s)

                    def late():
                        if not (isinstance(b, int) and b < 2):
                            add(L, B.prev().prev(), ST - 2)
                            add(L, B.prev().prev(), ST - 1)
                        if not first:
                            sames(L, B.prev())

                    scores(L, layer, B, late)
                    if not first:
                        begin(L, B.prev())
                    w(0)
                    if not last_:
                        fields(L, layer, B.next())
                    w(1)
                    ch = Chain(dve, L["soft"], SOFT)
                    ch.start(b)
                    dve.wait_ge(L["s_tr"], b + 1)
                    dve.wait_ge(L["ats_made"], b + 1)
                    wait(dve, L["soft"], SOFT * b)
                    ST_ = bank[6][:, 0:P]
                    ch.did(V.tensor_tensor_scan(scan1[:, :], ats[:, 0:P], ST_, -BIG, ALU.add, ALU.max))
                    ch.did(V.tensor_tensor_scan(scan2[:, P - 1::-1], ats[:, P:0:-1], ST_[:, P - 1::-1], -BIG,
                                                ALU.add, ALU.max))
                    V.tensor_reduce(v4[:, 0:1], ats[:, 1:P], AXX, ALU.min).then_inc(L["v4_made"], 1)
                    V.tensor_copy(v4[:, 1:2], ats[:, 0:1]).then_inc(L["v4_made"], 1)
                    w(2)
                    a(0)
                    w(3)
                    a(1)
                    w(4)
                    r = Chain(dve, L["row"], ROW)
                    r.start(b)
                    dve.wait_ge(L["rows_cp"], b + 1)
                    wait(dve, L["row"], ROW * b)
                    l_, f_, w_, a_ = [hc(rowS[:, k, :]) for k in range(4)]
                    r.did(V.tensor_tensor(hc(d0f[:, :])[:, :, 1:], w_[:, :, :CH - 1], a_[:, :, 1:], ALU.add))
                    r.did(V.tensor_tensor(hc(d1f[:, :])[:, :, 1:], l_[:, :, :CH - 1], a_[:, :, 1:], ALU.add))
                    r.did(V.tensor_tensor(hc(d1f[:, :])[:, :, 0], carry[:, :], a_[:, :, 0], ALU.add))
                    r.did(V.tensor_tensor(hc(d0b[:, :])[:, :, :CH - 1], w_[:, :, 1:], a_[:, :, 1:], ALU.add))
                    r.seq(V.tensor_tensor(hc(d1b[:, :])[:, :, :CH - 1], f_[:, :, 1:], a_[:, :, 1:], ALU.add))
                    r.did(V.tensor_tensor_scan(inr[:, :], d0f[:, :], d1f[:, :], -BIG, ALU.add, ALU.max))
                    r.seq(V.tensor_tensor_scan(outr[:, P - 1::-1], d0b[:, P - 1::-1], d1b[:, P - 1::-1], -BIG,
                                               ALU.add, ALU.max))
                    r.did(V.tensor_tensor(ct[:, 0, :], w_[:, :, CH - 1], hc(inr[:, :])[:, :, CH - 1], ALU.add))
                    r.seq(V.tensor_tensor(ct[:, 1, :], w_[:, :, 0], hc(outr[:, :])[:, :, 0], ALU.add))
                    r.did(V.tensor_tensor(carry[:, :], ct[:, 0, :], l_[:, :, CH - 1], ALU.max))
                    r.seq(V.tensor_tensor(ct[:, 2, :], ct[:, 1, :], f_[:, :, 0], ALU.max))
                    r.seq(V.tensor_tensor(ct[:, 3, :], ct[:, 2, :], hc(inr[:, :])[:, :, 0], ALU.max))
                    r.did(V.tensor_tensor(ct[:, 4, :], hc(d1f[:, :])[:, :, 0], ct[:, 3, :], ALU.subtract))
                    r.end()
                    a(2)
                    w(5)
                    a(3)
                    dve.wait_ge(L["cols_cp"], b + 1)
                    ch.seq(V.tensor_tensor_scan(scan1[:, :], ats[:, 0:P], ST_, cols[:, 0:1], ALU.add, ALU.max))
                    ch.did(V.tensor_tensor_scan(scan2[:, P - 1::-1], ats[:, P:0:-1], scan1[:, P - 1::-1],
                                                cols[:, 1:2], ALU.add, ALU.max))
                    dve.wait_ge(L["oh0_made"], b + 1)
                    ch.seq(V.tensor_scalar(rt[:, :], bank[7][:, 8:8 + H], -1.0, oh0[:, B.par:B.par + 1],
                                           ALU.add, ALU.mult))
                    ch.seq(V.tensor_scalar(rm[:, B.par, :], rt[:, :], 1.0, None, ALU.add))
                    ch.end()
                    w(6)
                    a(4)
                    dve.wait_ge(L["m_tr"], b + 1)
                    V.tensor_tensor(df[:, :], S[:, :], bank[6][:, P:2 * P], ALU.subtract).then_inc(L["dmade"], 1)
                    w(7)
                    a(5)

                z = blk_at(0, layer)
                fields(L, layer, z)
                blocks(dve, layer, turn)
                e = blk_at(NB - 1, layer)
                add(L, e.prev(), ST - 2)
                add(L, e.prev(), ST - 1)
                sames(L, e)
                begin(L, e)
                for s in range(ST):
                    weigh(L, layer, e, s)
                    if s:
                        add(L, e, s - 1)
                add(L, e, ST - 1)

            edge_phase(0)

            dve.wait_ge(S_["m_w"], 16 * 15)
            c1 = Chain(dve, L_[1]["init"], 99)
            c1.start(0)
            c1.did(V.memset(carry[:, :], -BIG))
            c1.did(V.memset(fo[:, 0:HV], 1.0))
            c1.sync()
            first_acc = V.memset(acc[:, 1, ST - 1, :], 0.0)
            c1.seq(first_acc)

            for c in range(2):
                for k, v in enumerate((v_al, v_ar)):
                    c1.seq(V.tensor_tensor(wtmp, w_ge[:, c, 0:D], v, ALU.mult))
                    c1.seq(V.tensor_reduce(w_ge[:, c, D + k * H:D + (k + 1) * H], hv(wtmp), AXX, ALU.add))
            dve.sem_inc(S_["m_wge"], 1)

            def stats(ch, k, src):
                ch.seq(V.bn_stats(st[:, k, :], src))
                dve.sem_inc(S_["stats_made"], 1)
                ch.seq(V.bn_aggr(mv[:, k, :], st[:, k, :]))
                V.tensor_scalar(vr[:, 2 * k:2 * k + 1], mv[:, k, 1:2], EPS, None, ALU.add).then_inc(S_[f"m_var{k}"], 1)

            def centre(ch, k, src, g, dst):
                ch.seq(V.scalar_tensor_tensor(dst, src, mv[:, k, 0:1], g, ALU.subtract, ALU.mult))

            def scale(ch, k, src, b, dst, n):
                dve.wait_ge(S_[f"m_rs{k}"], n + 1)
                ch.seq(V.scalar_tensor_tensor(dst, src, vr[:, 2 * k + 1:2 * k + 2], b, ALU.mult, ALU.add))

            def m_turn(t):
                if on(0, t):
                    ch = Chain(dve, S_["m_dve0"], M0)
                    ch.start(t)
                    dve.wait_ge(S_["m_acc"], 16 * (t + 1))
                    ch.seq(V.tensor_scalar(den[:, 0:H], hv(at_in)[:, :, HD], 1e-30, None, ALU.max))
                    ch.seq(V.reciprocal(den[:, H:2 * H], den[:, 0:H]))
                    wait(dve, S_["m_tr0"], t)
                    V.tensor_tensor(hv(at), hv(at_in)[:, :, 0:HD],
                                    den[:, H:2 * H].unsqueeze(2).to_broadcast([P, H, HD]),
                                    ALU.mult).then_inc(S_["m_rdacc"], 1)
                    ch.end()
                if on(3, t):
                    u = t - 3
                    ch = Chain(dve, S_["m_dve2"], M2)
                    ch.start(u)
                    dve.wait_ge(S_["m_mm1"], u + 1)
                    dve.wait_ge(S_["m_h1b"], u + 1)
                    ch.seq(V.tensor_tensor(z, bank[1][:, 0:D], h1b, ALU.add))
                    stats(ch, 2, z)
                    centre(ch, 2, z, v_g2, z2)
                if on(4, t):
                    dve.wait_ge(S_["m_tr3"], t - 3)
                    wait(dve, S_["m_sxh"], 16 * (t - 4))
                    V.tensor_tensor(xh, bank[5][:, D:2 * D], xm, ALU.add).then_inc(S_["m_dve3"], 1)
                    dve.wait_ge(S_["m_dve3"], t - 3)
                if on(3, t):
                    dve.wait_ge(S_["m_xb"], u + 1)
                    scale(ch, 2, z2, xb, xm, u)
                    stats(ch, 3, xm)
                if on(1, t):
                    c1_ = Chain(dve, S_["m_dve1"], M1)
                    c1_.start(t - 1)
                    dve.wait_ge(S_["m_mm0"], t)
                    dve.wait_ge(S_["m_hb"], t)
                    c1_.did(V.tensor_tensor(y, bank[0][:, 0:D], hb, ALU.add))
                if on(3, t):
                    dve.wait_ge(S_["m_rs3"], u + 1)
                    wait(dve, S_["m_tr2"], u)
                    ch.seq(V.tensor_scalar(h2, xm, mv[:, 3, 0:1], vr[:, 7:8], ALU.subtract, ALU.mult))
                    ch.end()
                if on(1, t):
                    c1_.sync()
                    stats(c1_, 1, y)
                    centre(c1_, 1, y, v_g1, y2)
                    wait(dve, S_["m_tr1"], t - 1)
                    wait(dve, S_["m_h1b"], t - 1)
                    scale(c1_, 1, y2, v_b1n, h1, t - 1)
                    c1_.end()

            m_turns(dve, m_turn)

            edge_phase(1)

            dve.wait_ge(S_["m_w"], 16 * 16)
            cf = Chain(dve, S_["f_dve"], FIN)

            def f_turn(t, k, lap):
                par = k % 2
                cf.start(t)
                dve.wait_ge(S_[f"f_in{k}"], 32 * (lap + 1))
                wait(dve, S_[f"f_st{par}"], 16 * (2 * lap + k // 2))
                a, d, o = fin_a[par], fin_d[par], fin_o[par]
                cf.seq(V.tensor_scalar(d[:, 0:H], hv(fin_in[k])[:, :, HD], 1e-30, None, ALU.max))
                cf.seq(V.reciprocal(d[:, H:2 * H], d[:, 0:H]))
                cf.seq(V.tensor_tensor(hv(a), hv(fin_in[k])[:, :, 0:HD],
                                       d[:, H:2 * H].unsqueeze(2).to_broadcast([P, H, HD]), ALU.mult))
                cf.seq(V.tensor_tensor(o, a, v_gb, ALU.add))
                cf.seq(V.scalar_tensor_tensor(a, o, 0.01, o, ALU.mult, ALU.max))
                cf.seq(V.tensor_tensor(o, a, fin_xh[k], ALU.add))
                cf.end()

            for t in range(4):
                f_turn(t, t, 0)
            with dve.Fori(1, NT // 4) as i:
                for k in range(4):
                    f_turn(4 * i + k, k, i)
            for t in range(NT // 4 * 4, NT):
                f_turn(t, t % 4, t // 4)


_W = ["L0_gnn_Wq", "L0_gnn_Wk", "L0_gnn_Wv", "L0_gnn_Wp", "L0_gnn_bp", "L0_gnn_ln1_g", "L0_gnn_ln1_b",
      "L0_gnn_ln2_g", "L0_gnn_ln2_b", "L0_gnn_W1", "L0_gnn_b1", "L0_gnn_W2", "L0_gnn_b2",
      "L1_gnn_W_lin", "L1_gnn_b_lin", "L1_gnn_W_gat", "L1_gnn_attn_l", "L1_gnn_attn_r", "L1_gnn_gat_bias"]


def kernel(**inputs):
    import numpy as np
    import concourse.bacc as bacc
    from concourse.bass_utils import run_bass_kernel_spmd as run

    a = {k: np.ascontiguousarray(v) for k, v in inputs.items()}
    x = np.concatenate([a["x"], np.zeros((NPAD - N, D), np.float32)])
    pad = NSPAN * SPAN - E
    i32 = lambda n, v: np.full(n, v, np.int32)
    src = np.concatenate([a["src"], i32(pad + SPAN, 0)])
    dst = np.concatenate([a["dst"], i32(pad, NPAD - 1), i32(SPAN, NOWHERE)])
    prev = np.concatenate([i32(1, -1), dst[:-1]])
    bias = np.concatenate([a["edge_weight1"].reshape(-1).view(np.int32), i32(pad + SPAN, 0)])
    edges = np.stack([src, dst, prev, bias], -1).reshape(NSPAN + 1, 2, P, 4).transpose(0, 2, 1, 3)
    last = np.concatenate([dst[:NSPAN * SPAN].reshape(NSPAN, SPAN)[:, -1], i32(LC * P - NSPAN, 1 << 30)])
    arrays = {"x": x, "last": last, "edges": np.ascontiguousarray(edges.reshape(-1, 8))}
    arrays.update({n: a[n].reshape(-1) if a[n].shape == (H, HD) else a[n] for n in _W})
    nc = bacc.Bacc("TRN2", target_bir_lowering=False, num_devices=1)
    args = [nc.dram_tensor(f"in_{n}", v.shape, mybir.dt.from_np(v.dtype), kind="ExternalInput").ap()
            for n, v in arrays.items()]
    o = nc.dram_tensor("out_0", (N, D), F32, kind="ExternalOutput").ap()
    build(nc, *args, o)
    r = run(nc, [{f"in_{n}": v for n, v in arrays.items()}], core_ids=[0])
    return r.results[0]["out_0"]
```
